# Optimizing a Trainium2 kernel written in Bass

```python
import numpy as np
import jax
import jax.numpy as jnp

def _softmax(x, axis=-1):
    return jax.nn.softmax(x, axis=axis)

def _gelu(x):
    return jax.nn.gelu(x, approximate=True)

def _silu(x):
    return jax.nn.silu(x)

def _sigmoid(x):
    return jax.nn.sigmoid(x)

def _layernorm(x, axis=-1, eps=1e-05):
    m = jnp.mean(x, axis=axis, keepdims=True)
    v = jnp.var(x, axis=axis, keepdims=True)
    return (x - m) / jnp.sqrt(v + eps)

def _scatter_add(tgt, idx, src, axis=0):
    return tgt.at[idx].add(src)

def _segment_sum(src, seg, n):
    return jax.ops.segment_sum(src, seg, n)
kernel_name = 'mk_gnn_preln_d1_gnn_r8_5aa3b3'

def setup_inputs(seed: int=0):
    np.random.seed(seed)
    _w = jnp.asarray

    def _rec_inputs():
        import jax
        import jax.numpy as jnp
        _gk = jax.random.key(seed)
        x = -0.000202 + 1 * jax.random.normal(jax.random.fold_in(_gk, 1), (6250, 128), jnp.float32)
        src = jax.random.randint(jax.random.fold_in(_gk, 2), (100000,), 0, 6250, jnp.int32)
        dst = jax.random.randint(jax.random.fold_in(_gk, 3), (100000,), 0, 6250, jnp.int32)
        _o = jnp.argsort(dst, stable=True)
        src = src[_o]
        dst = dst[_o]
        edge_attr_128 = -8.16379e-05 + 0.999858 * jax.random.normal(jax.random.fold_in(_gk, 12), (100000, 128), jnp.float32)
        return (x, src, dst, edge_attr_128)
    x, src, dst, edge_attr_128 = _rec_inputs()

    def _L0_gnn_setup():
        import jax, jax.numpy as jnp
        import numpy as np
        N_NODES = 6250
        N_EDGES = 100000
        NODE_DIM = 128
        EDGE_DIM = 128
        HIDDEN = 128
        HEADS = 8
        HEAD_DIM = HIDDEN // HEADS
        NEG_SLOPE = 0.2
        key = jax.random.key(seed)
        ks = jax.random.split(key, 16)
        s = 1.0 / np.sqrt(NODE_DIM)
        se = 1.0 / np.sqrt(EDGE_DIM)
        sm = 1.0 / np.sqrt(NODE_DIM + EDGE_DIM)
        return {'node_features': jax.random.normal(ks[0], (N_NODES, NODE_DIM), jnp.float32), 'edge_features': jax.random.normal(ks[1], (N_EDGES, EDGE_DIM), jnp.float32), 'src': jax.random.randint(ks[2], (N_EDGES,), 0, N_NODES, jnp.int32), 'dst': jax.random.randint(ks[3], (N_EDGES,), 0, N_NODES, jnp.int32), 'ni_w': jax.random.uniform(ks[4], (HIDDEN, NODE_DIM), jnp.float32, -s, s), 'ni_b': jax.random.uniform(ks[5], (HIDDEN,), jnp.float32, -s, s), 'nj_w': jax.random.uniform(ks[6], (HIDDEN, NODE_DIM), jnp.float32, -s, s), 'nj_b': jax.random.uniform(ks[7], (HIDDEN,), jnp.float32, -s, s), 'e_w': jax.random.uniform(ks[8], (HIDDEN, EDGE_DIM), jnp.float32, -se, se), 'e_b': jax.random.uniform(ks[9], (HIDDEN,), jnp.float32, -se, se), 'attn_proj': jax.random.normal(ks[10], (HEADS, HEAD_DIM), jnp.float32), 'msg_w': jax.random.uniform(ks[11], (NODE_DIM, NODE_DIM + EDGE_DIM), jnp.float32, -sm, sm), 'msg_b': jax.random.uniform(ks[12], (NODE_DIM,), jnp.float32, -sm, sm), 'out_w': jax.random.uniform(ks[13], (NODE_DIM, NODE_DIM), jnp.float32, -s, s), 'out_b': jax.random.uniform(ks[14], (NODE_DIM,), jnp.float32, -s, s)}
    _L0_gnn_all = _L0_gnn_setup()
    _L0_gnn_in = {k: v for k, v in _L0_gnn_all.items() if k in ('ni_w', 'ni_b', 'nj_w', 'nj_b', 'e_w', 'e_b', 'attn_proj', 'msg_w', 'msg_b', 'out_w', 'out_b')}
    del _L0_gnn_all
    return {'x': x, 'src': src, 'dst': dst, 'edge_attr_128': edge_attr_128, 'L0_gnn_ni_w': _L0_gnn_in['ni_w'], 'L0_gnn_ni_b': _L0_gnn_in['ni_b'], 'L0_gnn_nj_w': _L0_gnn_in['nj_w'], 'L0_gnn_nj_b': _L0_gnn_in['nj_b'], 'L0_gnn_e_w': _L0_gnn_in['e_w'], 'L0_gnn_e_b': _L0_gnn_in['e_b'], 'L0_gnn_attn_proj': _L0_gnn_in['attn_proj'], 'L0_gnn_msg_w': _L0_gnn_in['msg_w'], 'L0_gnn_msg_b': _L0_gnn_in['msg_b'], 'L0_gnn_out_w': _L0_gnn_in['out_w'], 'L0_gnn_out_b': _L0_gnn_in['out_b']}

def reference(x, src, dst, edge_attr_128, L0_gnn_ni_w, L0_gnn_ni_b, L0_gnn_nj_w, L0_gnn_nj_b, L0_gnn_e_w, L0_gnn_e_b, L0_gnn_attn_proj, L0_gnn_msg_w, L0_gnn_msg_b, L0_gnn_out_w, L0_gnn_out_b):
    import jax
    import jax.numpy as jnp

    def _L0_gnn_ref(node_features, edge_features, src, dst, ni_w, ni_b, nj_w, nj_b, e_w, e_b, attn_proj, msg_w, msg_b, out_w, out_b):
        import jax, jax.numpy as jnp
        import numpy as np
        N_NODES = 6250
        N_EDGES = 100000
        NODE_DIM = 128
        EDGE_DIM = 128
        HIDDEN = 128
        HEADS = 8
        HEAD_DIM = HIDDEN // HEADS
        NEG_SLOPE = 0.2
        E = src.shape[0]
        ni = node_features[src]
        nj = node_features[dst]
        hidden = ni @ ni_w.T + ni_b + (nj @ nj_w.T + nj_b) + (edge_features @ e_w.T + e_b)
        hidden = jnp.where(hidden >= 0, hidden, NEG_SLOPE * hidden)
        hidden = hidden.reshape(E, HEADS, HEAD_DIM)
        attn_logits = jnp.einsum('ehd,hd->eh', hidden, attn_proj)
        seg_max = jax.ops.segment_max(attn_logits, src, num_segments=N_NODES)
        ex = jnp.exp(attn_logits - seg_max[src])
        denom = jax.ops.segment_sum(ex, src, num_segments=N_NODES)
        attn_scores = ex / denom[src]
        messages = jnp.concatenate([nj, edge_features], axis=-1) @ msg_w.T + msg_b
        messages = messages.reshape(E, HEADS, HEAD_DIM) * attn_scores[..., None]
        agg = jax.ops.segment_sum(messages, src, num_segments=N_NODES)
        agg = agg.reshape(N_NODES, HEADS * HEAD_DIM)
        return agg @ out_w.T + out_b
    h = jnp.maximum(_layernorm(x, axis=-1), 0.0)
    x = x + _L0_gnn_ref(h, edge_attr_128, src, dst, L0_gnn_ni_w, L0_gnn_ni_b, L0_gnn_nj_w, L0_gnn_nj_b, L0_gnn_e_w, L0_gnn_e_b, L0_gnn_attn_proj, L0_gnn_msg_w, L0_gnn_msg_b, L0_gnn_out_w, L0_gnn_out_b)
    return x

_drawn_inputs = setup_inputs


def setup_inputs(seed=0):
    import zlib

    import numpy as np

    out = dict(_drawn_inputs(seed))
    spreads = {}
    factors = {'L0_gnn_ni_b': 8.0, 'L0_gnn_nj_b': 7.676, 'L0_gnn_e_b': 7.57, 'L0_gnn_msg_b': 2.804}
    for name, (base, spread) in spreads.items():
        noise = np.random.default_rng([zlib.crc32(name.encode()), seed]).standard_normal(out[name].shape)
        drawn = base * np.exp(spread * noise) if base else spread * noise
        out[name] = jnp.asarray(drawn.astype(out[name].dtype))
    for name, factor in factors.items():
        out[name] = (out[name] * factor).astype(out[name].dtype)
    return out
```

```python
from contextlib import ExitStack

import concourse.bass as bass
from concourse import mybir
from concourse.alu_op_type import AluOpType as ALU

F32 = mybir.dt.float32
BF16 = mybir.dt.bfloat16
I32 = mybir.dt.int32
ACT = mybir.ActivationFunctionType
AX = mybir.AxisListType
ds = bass.ds

P = 128
J = 4
GROUP = P * J
U = 2
NEG = -1.0e38
FAR = 1 << 20
LN_EPS = 1e-5
SLOPE = 0.2


class Plan:

    def __init__(self, n_nodes, n_edges, dim, heads):
        self.N, self.E, self.D, self.H = n_nodes, n_edges, dim, heads
        self.HD = dim // heads
        self.NT = -(-n_nodes // (P * U)) * U
        self.WHOLE_N = n_nodes // P
        self.REST_N = n_nodes - self.WHOLE_N * P
        full = -(-n_edges // GROUP)
        self.EG = -(-full // U) * U
        self.WHOLE = n_edges // GROUP
        self.REST = n_edges - self.WHOLE * GROUP
        self.EC = self.EG * J
        tiles = n_edges // P + self.NT
        self.SG = -(-tiles // (J * U)) * U
        self.ST = self.SG * J
        self.HALF = dim + 4
        self.ROW = 2 * self.HALF
        self.WM = dim + heads


class Tensors:
    pass


class Chain:

    def __init__(self, engine, sem):
        self.engine, self.sem, self.n = engine, sem, 0

    def then(self, instruction):
        self.n += 1
        instruction.then_inc(self.sem, 1)
        self.engine.wait_ge(self.sem, self.n)


def gnn_kernel(nc, x, src, dst, edge_attr, w_node, w_edge, w_out, ni_b, nj_b, e_b, msg_b, out_b,
               attn, out):
    N, D = x.shape
    E = src.shape[0]
    H = 8
    pl = Plan(N, E, D, H)
    with ExitStack() as whole:
        def sb(name, shape, dt=F32):
            return whole.enter_context(nc.sbuf_tensor(name, shape, dt))

        t = Tensors()
        t.x, t.src, t.dst, t.edge_attr, t.out = x, src, dst, edge_attr, out
        t.w_node_d, t.w_edge_d, t.w_out_d, t.attn_d, t.out_b_d = w_node, w_edge, w_out, attn, out_b
        t.ni_b, t.nj_b, t.e_b, t.msg_b = ni_b, nj_b, e_b, msg_b
        t.bm = nc.dram_tensor("dst_table", [pl.NT * P, 2 * D], F32).ap()
        t.rows = nc.dram_tensor("sorted_rows", [E + P, pl.ROW], F32).ap()
        t.tile_bucket_d = nc.dram_tensor("tile_bucket_d", [7 * P], I32).ap()
        t.tile_row_d = nc.dram_tensor("tile_row_d", [7 * P], I32).ap()
        t.tile_base_d = nc.dram_tensor("tile_base_d", [7 * P], F32).ap()
        t.psum = whole.enter_context(nc.psum_tensor("psum", [P, 8, 512], F32))
        t.node_a = sb("node_a", [P, pl.NT * D])
        t.nodes_flat = sb("nodes", [P, pl.NT * pl.WM])
        t.nodes = t.nodes_flat[:, :].rearrange("p (t f) -> p t f", t=pl.NT)
        t.shared = sb("shared", [P, 3 * pl.ST * H])
        t.hot = t.shared[:, 0:pl.EC * pl.NT // 2].bitcast(BF16).rearrange(
            "p (c b) -> p c b", b=pl.NT)
        t.logits = t.shared[:, 0:pl.ST * H]
        t.tile_max = t.shared[:, pl.ST * H:2 * pl.ST * H].rearrange("p (h t) -> p h t", h=H)
        t.node_max = t.shared[:, 2 * pl.ST * H:3 * pl.ST * H].rearrange("p (h t) -> p h t", h=H)
        t.ident = sb("ident", [P, P])
        t.ones = sb("ones", [P, P])
        t.ones_bf = sb("ones_bf", [P, P], BF16)
        t.before_bf = sb("before_bf", [P, P], BF16)
        t.lane = sb("lane", [P, P])
        t.id1 = sb("id1", [P, pl.EC])
        t.pad_off = sb("pad_off", [P, pl.EC])
        t.dst_i = sb("dst_i", [P, pl.EC + U * J], I32)
        t.start = sb("start", [P, pl.NT])
        t.tile_base = sb("tile_base", [P, pl.ST])
        t.tile_bucket = sb("tile_bucket", [1, pl.ST], I32)
        t.tile_row = sb("tile_row", [1, pl.ST], I32)
        t.rel = sb("rel", [P, pl.ST])
        t.w_edge = sb("w_edge", [P, 2 * D])
        t.w_out = sb("w_out", [P, D])
        t.attn = sb("attn", [P, D])
        t.out_bias = sb("out_bias", [P, D])
        tables(nc, pl, t)
        buckets(nc, pl, t)
        edges(nc, pl, t)
        logits(nc, pl, t)
        maxima(nc, pl, t)
        sums(nc, pl, t)
        output(nc, pl, t)


def repeat(engine, n, body):
    body(0)
    with engine.Fori(1, n) as i:
        body(i)


def wait_used(engine, semaphore, value):
    if not (isinstance(value, int) and value == 0):
        engine.wait_ge(semaphore, value)


def held(engine, register, i, k):
    if isinstance(i, int):
        return i + k
    engine.reg_add(register, i, k)
    return engine.snap(register)


def over(ap, n):
    return ap.unsqueeze(2).to_broadcast([ap.shape[0], ap.shape[1], n])


def under(ap, n):
    return ap.unsqueeze(1).to_broadcast([ap.shape[0], n, ap.shape[1]])


def tables(nc, pl, t):
    D, NT = pl.D, pl.NT
    META = pl.EG // 2
    with ExitStack() as ctx:
        def sb(name, shape, dt=F32):
            return ctx.enter_context(nc.sbuf_tensor(name, shape, dt))

        def sem(name):
            return ctx.enter_context(nc.semaphore(name))

        w_node = sb("w_node", [P, 3 * D])
        bias = sb("bias", [P, 3 * D])
        bias_in = sb("bias_in", [P, 2, D])
        stats = sb("stats", [P, U, 6])
        moments = sb("moments", [P, U, 2])
        mean_var = sb("mean_var", [P, NT * 2])
        std = sb("std", [P, NT])
        rstd = sb("rstd", [P, NT])
        eps = sb("eps", [P, 1])
        normed = sb("normed", [P, U, D])
        h_t = sb("h_t", [P, U, D])
        bm_out = sb("bm_out", [P, U, 2 * D])
        meta_i = sb("meta_i", [META, 2, 2, GROUP], I32)
        meta_f = sb("meta_f", [META, 2, 2, GROUP])
        src_f = sb("src_f", [P, pl.EC])
        src_i = sb("src_i", [P, pl.EC], I32)
        hi_i = sb("hi_i", [P, pl.EC], I32)
        hi_bf = sb("hi_bf", [P, pl.EC], BF16)
        lane_bf = sb("lane_bf", [P, P], BF16)
        zero_row = sb("zero_row", [P, pl.ROW])

        cleared = sem("cleared")
        x_loaded = sem("x_loaded")
        meta_loaded = sem("meta_loaded")
        weights_loaded = sem("weights_loaded")
        bias_loaded = sem("bias_loaded")
        consts_ready = sem("consts_ready")
        pool_chain = sem("pool_chain")
        dve_chain = sem("dve_chain")
        stats_ready = [sem(f"stats_ready{u}") for u in range(U)]
        moments_ready = [sem(f"moments_ready{u}") for u in range(U)]
        var_ready = [sem(f"var_ready{u}") for u in range(U)]
        std_ready = sem("std_ready")
        rstd_ready = sem("rstd_ready")
        bias_ready = sem("bias_ready")
        meta_cast = sem("meta_cast")
        meta_turned = sem("meta_turned")
        meta_copied = sem("meta_copied")
        normed_ready = [sem(f"normed_ready{u}") for u in range(U)]
        turned = [sem(f"turned{u}") for u in range(U)]
        h_ready = [sem(f"h_ready{u}") for u in range(U)]
        projected = [sem(f"projected{u}") for u in range(U)]
        bm_ready = [sem(f"bm_ready{u}") for u in range(U)]
        bm_stored = [sem(f"bm_stored{u}") for u in range(U)]
        slack_stored = sem("slack_stored")
        xs = t.nodes[:, :, 0:D]
        turn_ps = [t.psum[:, u, 0:D] for u in range(U)]
        proj_ps = [t.psum[:, 2 + u, 0:3 * D] for u in range(U)]
        meta_ps = [t.psum[:, 4 + k, 0:J * META].rearrange("p (j g) -> p j g", j=J)
                   for k in range(4)]

        with nc.Block() as block:
            @block.sync
            def _(sp):
                sp.wait_ge(cleared, 4)
                whole0 = min(META, pl.WHOLE)
                whole1 = pl.WHOLE - whole0
                for k, ids in enumerate((t.src, t.dst)):
                    sp.dma_start(meta_i[0:whole0, k, 0, :], ids[0:whole0 * GROUP].rearrange(
                        "(g c) -> g c", c=GROUP)).then_inc(meta_loaded, 16)
                    sp.dma_start(meta_i[0:whole1, k, 1, :],
                                 ids[whole0 * GROUP:pl.WHOLE * GROUP].rearrange(
                                     "(g c) -> g c", c=GROUP)).then_inc(meta_loaded, 16)
                    sp.dma_start(meta_i[whole1:whole1 + 1, k, 1, 0:pl.REST],
                                 ids[pl.WHOLE * GROUP:pl.E].rearrange(
                                     "(g c) -> g c", g=1)).then_inc(meta_loaded, 16)
                sp.dma_start(xs[:, 0:pl.WHOLE_N, :], t.x[0:pl.WHOLE_N * P, :].rearrange(
                    "(t p) f -> p t f", p=P)).then_inc(x_loaded, 16)
                sp.dma_start(xs[0:pl.REST_N, pl.WHOLE_N, :],
                             t.x[pl.WHOLE_N * P:pl.N, :]).then_inc(x_loaded, 16)
                sp.dma_start(t.rows[pl.E:pl.E + P, :], zero_row[:, :]).then_inc(slack_stored, 16)
                def body(i):
                    for u in range(U):
                        sp.wait_ge(bm_ready[u], i + 1)
                        sp.dma_start(t.bm[ds((i * U + u) * P, P), :],
                                     bm_out[:, u, :]).then_inc(bm_stored[u], 16)
                repeat(sp, NT // U, body)
                for u in range(U):
                    sp.wait_ge(bm_stored[u], 16 * (NT // U))
                sp.wait_ge(slack_stored, 16)

            @block.gpsimd
            def _(pool):
                chain = Chain(pool, pool_chain)
                nc.gpsimd.memset(meta_i[:, 0, :, :], NT * P).then_inc(cleared, 1)
                nc.gpsimd.memset(meta_i[:, 1, :, :], 0).then_inc(cleared, 1)
                nc.gpsimd.memset(xs[:, pl.WHOLE_N:NT, :], 0.0).then_inc(cleared, 1)
                nc.gpsimd.memset(zero_row[:, :], 0.0).then_inc(cleared, 1)
                chain.then(nc.gpsimd.memset(t.ones[:, :], 1.0))
                nc.gpsimd.memset(t.ones_bf[:, :], 1.0)
                nc.gpsimd.iota(t.lane[:, :], [[1, P]], base=0, channel_multiplier=0,
                               allow_small_or_imprecise_dtypes=True)
                nc.gpsimd.iota(lane_bf[:, :], [[1, P]], base=0, channel_multiplier=0,
                               allow_small_or_imprecise_dtypes=True)
                nc.gpsimd.affine_select(out=t.ident[:, :], in_=t.ones[:, :], pattern=[[1, P]],
                                        compare_op=ALU.is_equal, fill=0.0, base=0,
                                        channel_multiplier=-1)
                nc.gpsimd.affine_select(out=t.before_bf[:, :], in_=t.ones[:, :],
                                        pattern=[[1, P]], compare_op=ALU.is_gt, fill=0.0, base=0,
                                        channel_multiplier=-1).then_inc(consts_ready, 1)

            @block.scalar
            def _(act):
                act.dma_start(w_node[:, :], t.w_node_d).then_inc(weights_loaded, 16)
                act.dma_start(t.w_edge[:, :], t.w_edge_d).then_inc(weights_loaded, 16)
                act.dma_start(t.w_out[:, :], t.w_out_d).then_inc(weights_loaded, 16)
                act.dma_start(t.attn[:, :], t.attn_d.partition_broadcast(P)).then_inc(weights_loaded, 16)
                act.dma_start(t.out_bias[:, :], t.out_b_d.partition_broadcast(P)).then_inc(weights_loaded, 16)
                act.dma_start(bias[:, 0:D], t.ni_b.partition_broadcast(P)).then_inc(bias_loaded, 16)
                act.dma_start(bias[:, 2 * D:3 * D], t.msg_b.partition_broadcast(P)).then_inc(bias_loaded, 16)
                act.dma_start(bias_in[:, 0, :], t.nj_b.partition_broadcast(P)).then_inc(bias_loaded, 16)
                act.dma_start(bias_in[:, 1, :], t.e_b.partition_broadcast(P)).then_inc(bias_loaded, 16)
                for u in range(U):
                    act.wait_ge(var_ready[u], NT // U)
                nc.scalar.activation(std[:, :], mean_var[:, 1:2 * NT:2], ACT.Sqrt,
                                     bias=eps[:, :]).then_inc(std_ready, 1)
                def body(i):
                    for u in range(U):
                        act.wait_ge(turned[u], i + 1)
                        wait_used(act, projected[u], i)
                        nc.scalar.activation(h_t[:, u, :], turn_ps[u],
                                             ACT.Relu).then_inc(h_ready[u], 1)
                repeat(act, NT // U, body)
                act.wait_ge(weights_loaded, 16 * 5)

            @block.tensor
            def _(pe):
                pe.wait_ge(consts_ready, 1)
                pe.wait_ge(meta_cast, 1)
                for k in range(2):
                    for half in range(2):
                        for j in range(J):
                            last = nc.tensor.transpose(meta_ps[2 * k + half][:, j, :],
                                                       meta_f[:, k, half, j:GROUP:J],
                                                       t.ident[0:META, 0:META])
                        last.then_inc(meta_turned, 1)
                pe.wait_ge(weights_loaded, 16 * 5)

                def body(i):
                    for u in range(U):
                        pe.wait_ge(normed_ready[u], i + 1)
                        wait_used(pe, h_ready[u], i)
                        nc.tensor.transpose(turn_ps[u], normed[:, u, :],
                                            t.ident[:, :]).then_inc(turned[u], 1)
                    for u in range(U):
                        pe.wait_ge(h_ready[u], i + 1)
                        wait_used(pe, bm_ready[u], i)
                        nc.tensor.matmul(proj_ps[u], h_t[:, u, :], w_node[:, :],
                                         start=True, stop=True).then_inc(projected[u], 1)
                repeat(pe, NT // U, body)

            @block.vector
            def _(dve):
                chain = Chain(dve, dve_chain)
                nc.vector.memset(eps[:, :], LN_EPS)
                chain.then(nc.vector.memset(t.dst_i[:, :], 0))
                dve.wait_ge(meta_loaded, 16 * 6)
                nc.vector.tensor_copy(meta_f[:, :, :, :].rearrange("g k h c -> g (k h c)"),
                                      meta_i[:, :, :, :].rearrange("g k h c -> g (k h c)")).then_inc(meta_cast, 1)
                dve.wait_ge(x_loaded, 32)
                reg = dve.alloc_register("after")
                def body(i):
                    after = held(dve, reg, i, 1)
                    for u in range(U):
                        wait_used(dve, moments_ready[u], i)
                        nc.vector.bn_stats(stats[:, u, :], t.nodes_flat[:, ds((i * U + u) * pl.WM, D)]
                                           ).then_inc(stats_ready[u], 1)
                    for u in range(U):
                        dve.wait_ge(x_loaded, 32)
                        dve.wait_ge(stats_ready[u], after)
                        wait_used(dve, var_ready[u], i)
                        nc.vector.bn_aggr(moments[:, u, :], stats[:, u, :]).then_inc(moments_ready[u], 1)
                    for u in range(U):
                        dve.wait_ge(moments_ready[u], i + 1)
                        nc.vector.tensor_copy(mean_var[:, ds((i * U + u) * 2, 2)],
                                              moments[:, u, :]).then_inc(var_ready[u], 1)
                repeat(dve, NT // U, body)
                for k in range(2):
                    for half in range(2):
                        dve.wait_ge(meta_turned, 2 * k + half + 1)
                        to = (src_f if k == 0 else t.dst_i)[:, 0:pl.EC].rearrange(
                            "p (g j) -> p j g", j=J)[:, :, half * META:(half + 1) * META]
                        last = nc.vector.tensor_copy(to, meta_ps[2 * k + half])
                chain.then(last)
                nc.vector.tensor_scalar(t.id1[:, :], src_f[:, :], 1.0, None, ALU.add)
                nc.vector.tensor_scalar(t.pad_off[:, :], src_f[:, :], float(NT * P), float(FAR),
                                        ALU.is_ge, ALU.mult)
                chain.then(nc.vector.tensor_copy(src_i[:, :], src_f[:, :]))
                chain.then(nc.vector.tensor_scalar(hi_i[:, :], src_i[:, :], 7, None,
                                                   ALU.arith_shift_right))
                chain.then(nc.vector.tensor_copy(hi_bf[:, :], hi_i[:, :]))
                dve.wait_ge(bias_loaded, 16 * 4)
                chain.then(nc.vector.tensor_tensor(bias[:, 0:D], bias[:, 0:D], bias_in[:, 0, :], ALU.add))
                chain.then(nc.vector.tensor_tensor(bias[:, 0:D], bias[:, 0:D], bias_in[:, 1, :], ALU.add))
                chain.then(nc.vector.memset(bias[:, D:2 * D], 0.0))
                dve.wait_ge(std_ready, 1)
                chain.then(nc.vector.reciprocal(rstd[:, :], std[:, :]))

                def body(i):
                    for u in range(U):
                        it = i * U + u
                        wait_used(dve, turned[u], i)
                        nc.vector.tensor_scalar(normed[:, u, :], t.nodes_flat[:, ds(it * pl.WM, D)],
                                                mean_var[:, ds(it * 2, 1)], rstd[:, ds(it, 1)],
                                                ALU.subtract, ALU.mult).then_inc(normed_ready[u], 1)
                    for u in range(U):
                        it = i * U + u
                        dve.wait_ge(projected[u], i + 1)
                        wait_used(dve, bm_stored[u], i * 16)
                        nc.vector.tensor_tensor(t.node_a[:, ds(it * D, D)], proj_ps[u][:, 0:D],
                                                bias[:, 0:D], ALU.add)
                        nc.vector.tensor_tensor(bm_out[:, u, :], proj_ps[u][:, D:3 * D],
                                                bias[:, D:3 * D], ALU.add).then_inc(bm_ready[u], 1)
                repeat(dve, NT // U, body)
                dve.wait_ge(consts_ready, 1)
                step = pl.EC // 8
                for c in range(0, pl.EC, step):
                    nc.vector.tensor_tensor(t.hot[:, c:c + step, :],
                                            over(hi_bf[:, c:c + step], NT),
                                            under(lane_bf[:, 0:NT], step), ALU.is_equal)


def buckets(nc, pl, t):
    NT, ST = pl.NT, pl.ST
    C = 7
    CH = 8
    with ExitStack() as ctx:
        def sb(name, shape, dt=F32):
            return ctx.enter_context(nc.sbuf_tensor(name, shape, dt))

        def sem(name):
            return ctx.enter_context(nc.semaphore(name))

        count = sb("count", [P, NT])
        tiles_i = sb("tiles_i", [P, NT], I32)
        tiles = sb("tiles", [P, NT])
        ends = sb("ends", [P, NT])
        tile_start = sb("tile_start", [P, NT])
        tile_id = sb("tile_id", [P, C])
        pairs = sb("pairs", [P, C, NT])
        chosen = sb("chosen", [P, C, NT])
        bucket = sb("bucket", [P, C])
        first_tile = sb("first_tile", [P, C])
        first_row = sb("first_row", [P, C])
        row = sb("row", [P, C])
        row_i = sb("row_i", [P, C], I32)
        bucket_i = sb("bucket_i", [P, C], I32)
        base = sb("base", [P, C])
        counted = sem("counted")
        ids_ready = sem("ids_ready")
        order = sem("bucket_order")
        found = sem("tiles_found")
        stored = sem("tiles_stored")
        loaded = sem("tiles_loaded")
        hist = t.psum[:, 0, 0:CH * NT]

        with nc.Block() as block:
            @block.tensor
            def _(pe):
                rhs = t.hot[:, :, :].rearrange("p c b -> p (c b)")
                n = pl.EC // CH
                nc.tensor.matmul(hist, t.ones_bf[:, :], rhs[:, 0:CH * NT], start=True, stop=False)
                with pe.Fori(1, n - 1) as i:
                    nc.tensor.matmul(hist, t.ones_bf[:, :], rhs[:, ds(i * (CH * NT), CH * NT)],
                                     start=False, stop=False)
                nc.tensor.matmul(hist, t.ones_bf[:, :], rhs[:, (n - 1) * CH * NT:n * CH * NT],
                                 start=False, stop=True).then_inc(counted, 1)

            @block.gpsimd
            def _(pool):
                nc.gpsimd.iota(tile_id[:, :], [[P, C]], base=0, channel_multiplier=1,
                               allow_small_or_imprecise_dtypes=True).then_inc(ids_ready, 1)

            @block.vector
            def _(dve):
                chain = Chain(dve, order)
                v = nc.vector
                dve.wait_ge(counted, 1)
                chain.then(v.tensor_reduce(count[:, :], hist.rearrange("p (c b) -> p b c", c=CH),
                                           AX.X, ALU.add))
                chain.then(v.tensor_scalar(tiles[:, :], count[:, :], float(P - 1), None, ALU.add))
                chain.then(v.tensor_copy(tiles_i[:, :], tiles[:, :]))
                chain.then(v.tensor_scalar(tiles_i[:, :], tiles_i[:, :], 7, None, ALU.arith_shift_right))
                chain.then(v.tensor_copy(tiles[:, :], tiles_i[:, :]))
                chain.then(v.tensor_tensor_scan(ends[:, :], t.ones[:, 0:NT], count[:, :], 0.0,
                                                ALU.mult, ALU.add))
                chain.then(v.tensor_tensor(t.start[:, :], ends[:, :], count[:, :], ALU.subtract))
                chain.then(v.tensor_tensor_scan(ends[:, :], t.ones[:, 0:NT], tiles[:, :], 0.0,
                                                ALU.mult, ALU.add))
                chain.then(v.tensor_tensor(tile_start[:, :], ends[:, :], tiles[:, :], ALU.subtract))
                dve.wait_ge(ids_ready, 1)
                chain.then(v.tensor_tensor(pairs[:, :, :], over(tile_id[:, :], NT),
                                           under(tile_start[:, :], C), ALU.is_ge))
                chain.then(v.tensor_reduce(bucket[:, :], pairs[:, :, :], AX.X, ALU.add))
                chain.then(v.tensor_scalar(bucket[:, :], bucket[:, :], -1.0, None, ALU.add))
                chain.then(v.tensor_tensor(pairs[:, :, :], over(bucket[:, :], NT),
                                           under(t.lane[:, 0:NT], C), ALU.is_equal))
                chain.then(v.tensor_tensor(chosen[:, :, :], pairs[:, :, :],
                                           under(tile_start[:, :], C), ALU.mult))
                chain.then(v.tensor_reduce(first_tile[:, :], chosen[:, :, :], AX.X, ALU.add))
                chain.then(v.tensor_tensor(chosen[:, :, :], pairs[:, :, :],
                                           under(t.start[:, :], C), ALU.mult))
                chain.then(v.tensor_reduce(first_row[:, :], chosen[:, :, :], AX.X, ALU.add))
                chain.then(v.tensor_tensor(row[:, :], tile_id[:, :], first_tile[:, :], ALU.subtract))
                chain.then(v.scalar_tensor_tensor(row[:, :], row[:, :], float(P), first_row[:, :],
                                                  ALU.mult, ALU.add))
                chain.then(v.tensor_scalar(row[:, :], row[:, :], float(pl.E), None, ALU.min))
                chain.then(v.tensor_copy(row_i[:, :], row[:, :]))
                chain.then(v.tensor_copy(bucket_i[:, :], bucket[:, :]))
                chain.then(v.tensor_scalar(base[:, :], bucket[:, :], float(P), 1.0, ALU.mult, ALU.add))
                v.tensor_copy(base[:, :], base[:, :]).then_inc(found, 1)

            @block.sync
            def _(sp):
                sp.wait_ge(found, 1)
                with nc.allow_non_contiguous_dma("900 numbers"):
                    for to, of in ((t.tile_row_d, row_i), (t.tile_bucket_d, bucket_i),
                                   (t.tile_base_d, base)):
                        sp.dma_start(to.rearrange("(c p) -> p c", p=P), of[:, :]).then_inc(stored, 16)
                sp.wait_ge(stored, 48)
                sp.dma_start(t.tile_row[:, :], t.tile_row_d[0:ST].rearrange(
                    "(a n) -> a n", a=1)).then_inc(loaded, 16)
                sp.dma_start(t.tile_bucket[:, :], t.tile_bucket_d[0:ST].rearrange(
                    "(a n) -> a n", a=1)).then_inc(loaded, 16)
                sp.dma_start(t.tile_base[:, :], t.tile_base_d[0:ST].partition_broadcast(P)).then_inc(loaded, 16)
                sp.wait_ge(loaded, 48)


def edges(nc, pl, t):
    D, NT, H2 = pl.D, pl.NT, pl.HALF
    N_IT = pl.EG // U
    JN = J * NT
    with ExitStack() as ctx:
        def sb(name, shape, dt=F32):
            return ctx.enter_context(nc.sbuf_tensor(name, shape, dt))

        def sem(name):
            return ctx.enter_context(nc.semaphore(name))

        def sems(name):
            return [sem(f"{name}{u}") for u in range(U)]

        feat = sb("feat", [P, U, J * D])
        feat_t = sb("feat_t", [P, U, J * P])
        got = sb("got", [P, U, J * 2 * D])
        rows = sb("rows", [P, U, J * pl.ROW])
        dst_now = sb("dst_now", [P, U, J], I32)
        place = sb("place", [P, U, J], I32)
        place_f = sb("place_f", [P, U, J])
        rank = sb("rank", [P, U, JN])
        group_hot = sb("group_hot", [P, U, NT])
        before = sb("before", [P, U, NT])
        feat_loaded, turned, turned_copied, multiplied = map(
            sems, ("feat_loaded", "feat_turned", "feat_t_ready", "product_ready"))
        gathered, dst_ready, ranked, picked, place_sum, place_num, place_ready = map(
            sems, ("gathered", "dst_ready", "ranked", "picked", "place_sum", "place_num", "place_ready"))
        hot_summed, before_ready, rows_ready, scattered = map(
            sems, ("hot_summed", "before_ready", "rows_ready", "scattered"))
        rows_cleared = sem("rows_cleared")
        turn_ps = [t.psum[:, u, :] for u in range(U)]
        prod_ps = [t.psum[:, 2 + 2 * u:4 + 2 * u, :] for u in range(U)]
        rank_ps = [t.psum[:, 6 + u, 0:JN] for u in range(U)]
        hot = t.hot.rearrange("p c b -> p (c b)")
        feat_d = t.edge_attr[0:pl.WHOLE * GROUP, :].rearrange("(g p j) f -> g p (j f)", p=P, j=J)
        rest_p = pl.REST // J

        with nc.Block() as block:
            @block.sync
            def _(sp):
                def body(i):
                    for u in range(U):
                        wait_used(sp, turned[u], i)
                        sp.dma_start(feat[:, u, :], feat_d[ds(i * U + u, 1), :, :].rearrange(
                            "a p f -> (a p) f")).then_inc(feat_loaded[u], 16)
                repeat(sp, N_IT - 1, body)
                for u in range(U):
                    g = (N_IT - 1) * U + u
                    sp.wait_ge(turned[u], N_IT - 1)
                    if g < pl.WHOLE:
                        sp.dma_start(feat[:, u, :], feat_d[g, :, :]).then_inc(feat_loaded[u], 16)
                    else:
                        sp.dma_start(feat[0:rest_p, u, :], t.edge_attr[g * GROUP:pl.E, :].rearrange(
                            "(p j) f -> p (j f)", j=J)).then_inc(feat_loaded[u], 16)

            @block.gpsimd
            def _(pool):
                last_node = pool.to_reg(NT * P - 1)
                last_row = pool.to_reg(pl.E - 1)
                regs = [pool.alloc_register(n) for n in ("after", "after2")]

                def gather(i, after, u):
                    pool.wait_ge(rows_cleared, 1)
                    pool.wait_ge(dst_ready[u], after)
                    wait_used(pool, rows_ready[u], i)
                    for j in range(J):
                        nc.gpsimd.indirect_dma_start(
                            out=got[:, u, j * 2 * D:(j + 1) * 2 * D], out_offset=None,
                            in_=t.bm[:, :],
                            in_offset=bass.IndirectOffsetOnAxis(ap=dst_now[:, u, j:j + 1], axis=0),
                            bounds_check=last_node, oob_is_err=False).then_inc(gathered[u], 16)

                def scatter(after, u):
                    pool.wait_ge(rows_cleared, 1)
                    pool.wait_ge(place_ready[u], after)
                    pool.wait_ge(rows_ready[u], after)
                    for j in range(J):
                        nc.gpsimd.indirect_dma_start(
                            out=t.rows[:, :],
                            out_offset=bass.IndirectOffsetOnAxis(ap=place[:, u, j:j + 1], axis=0),
                            in_=rows[:, u, j * pl.ROW:(j + 1) * pl.ROW], in_offset=None,
                            bounds_check=last_row, oob_is_err=False).then_inc(scattered[u], 16)

                nc.gpsimd.memset(rows[:, :, :], 0.0).then_inc(rows_cleared, 1)
                gather(0, 1, 0)
                def body(i):
                    after, after2 = held(pool, regs[0], i, 1), held(pool, regs[1], i, 2)
                    gather(i, after, 1)
                    scatter(after, 0)
                    gather(after, after2, 0)
                    scatter(after, 1)
                repeat(pool, N_IT - 1, body)
                gather(N_IT - 1, N_IT, 1)
                scatter(N_IT, 0)
                scatter(N_IT, 1)
                for u in range(U):
                    pool.wait_ge(scattered[u], 16 * J * N_IT)

            @block.scalar
            def _(act):
                def body(i):
                    for u in range(U):
                        act.wait_ge(turned[u], i + 1)
                        wait_used(act, multiplied[u], i)
                        nc.scalar.copy(feat_t[:, u, :], turn_ps[u]).then_inc(turned_copied[u], 1)
                repeat(act, N_IT, body)

            @block.tensor
            def _(pe):
                def body(i):
                    for u in range(U):
                        pe.wait_ge(feat_loaded[u], i * 16 + 16)
                        wait_used(pe, turned_copied[u], i)
                        for j in range(J):
                            last = nc.tensor.transpose(turn_ps[u][:, j * P:(j + 1) * P],
                                                       feat[:, u, j * D:(j + 1) * D], t.ident[:, :])
                        last.then_inc(turned[u], 1)
                    for u in range(U):
                        c0 = (i * U + u) * JN
                        pe.wait_ge(before_ready[u], i + 1)
                        wait_used(pe, picked[u], i)
                        nc.tensor.matmul(rank_ps[u], t.before_bf[:, :], hot[:, ds(c0, JN)],
                                         start=True, stop=False)
                        for j in range(J - 1):
                            for k in range(j + 1, J):
                                nc.tensor.matmul(rank_ps[u][:, k * NT:(k + 1) * NT], t.ones_bf[:, :],
                                                 hot[:, ds(c0 + j * NT, NT)], start=False, stop=False)
                        for j in range(J):
                            last = nc.tensor.matmul(rank_ps[u][:, j * NT:(j + 1) * NT], t.ones[:, :],
                                                    before[:, u, :], start=False, stop=j == J - 1)
                        last.then_inc(ranked[u], 1)
                    for u in range(U):
                        pe.wait_ge(turned_copied[u], i + 1)
                        wait_used(pe, rows_ready[u], i)
                        for j in range(J):
                            last = nc.tensor.matmul(
                                prod_ps[u][:, j // 2, (j % 2) * 2 * D:(j % 2 + 1) * 2 * D],
                                feat_t[:, u, j * P:(j + 1) * P], t.w_edge[:, :], start=True, stop=True)
                        last.then_inc(multiplied[u], 1)
                repeat(pe, N_IT, body)

            @block.vector
            def _(dve):
                v = nc.vector
                v.tensor_scalar(before[:, 0, :], t.start[:, :], 1.0 / P, None,
                                ALU.mult).then_inc(before_ready[0], 1)
                for u in range(U):
                    v.tensor_copy(dst_now[:, u, :], t.dst_i[:, u * J:(u + 1) * J]).then_inc(dst_ready[u], 1)
                dve.wait_ge(rows_cleared, 1)
                def body(i):
                    for u in range(U):
                        nxt, more = (u + 1) % U, (u + 1) // U
                        col = (i * U + u) * J
                        wait_used(dve, ranked[nxt], i + more)
                        v.tensor_reduce(group_hot[:, u, :], hot[:, ds(col * NT, JN)].rearrange(
                            "p (j b) -> p b j", j=J), AX.X, ALU.add).then_inc(hot_summed[u], 1)
                        dve.wait_ge(hot_summed[u], i + 1)
                        dve.wait_ge(before_ready[u], i + 1)
                        v.tensor_tensor(before[:, nxt, :], before[:, u, :], group_hot[:, u, :],
                                        ALU.add).then_inc(before_ready[nxt], 1)
                    for u in range(U):
                        col = (i * U + u) * J
                        dve.wait_ge(ranked[u], i + 1)
                        v.tensor_tensor(rank[:, u, :], rank_ps[u], hot[:, ds(col * NT, JN)],
                                        ALU.mult).then_inc(picked[u], 1)
                        dve.wait_ge(picked[u], i + 1)
                        v.tensor_reduce(place_f[:, u, :], rank[:, u, :].rearrange(
                            "p (j b) -> p j b", j=J), AX.X, ALU.add).then_inc(place_sum[u], 1)
                        dve.wait_ge(place_sum[u], i + 1)
                        wait_used(dve, scattered[u], i * (16 * J))
                        v.tensor_tensor(place[:, u, :], place_f[:, u, :], t.pad_off[:, ds(col, J)],
                                        ALU.add).then_inc(place_ready[u], 1)
                        v.tensor_copy(rows[:, u, D:J * pl.ROW:pl.ROW], t.id1[:, ds(col, J)])
                        dve.wait_ge(multiplied[u], i + 1)
                        dve.wait_ge(gathered[u], i * (16 * J) + 16 * J)
                        v.tensor_tensor(
                            rows[:, u, :].rearrange("p (k f) -> p k f", f=H2)[:, :, 0:D],
                            prod_ps[u].rearrange("p b (k f) -> p (b k) f", f=D),
                            got[:, u, :].rearrange("p (k f) -> p k f", f=D),
                            ALU.add).then_inc(rows_ready[u], 1)
                        v.tensor_copy(dst_now[:, u, :], t.dst_i[:, ds(col + U * J, J)]).then_inc(dst_ready[u], 1)
                repeat(dve, N_IT, body)


def load_tiles(nc, pl, t, sp, i, u, to, first, width, loaded):
    for j in range(J):
        row = sp.value_load(t.tile_row[0:1, ds((i * U + u) * J + j, 1)], min_val=0, max_val=pl.E)
        sp.dma_start(to[:, u, j * width:(j + 1) * width],
                     t.rows[ds(row, P), first:first + width]).then_inc(loaded[u], 16)


def logits(nc, pl, t):
    D, H, HD, H2 = pl.D, pl.H, pl.HD, pl.HALF
    N_IT = pl.SG // U
    with ExitStack() as ctx:
        def sb(name, shape, dt=F32):
            return ctx.enter_context(nc.sbuf_tensor(name, shape, dt))

        def sems(name):
            return [ctx.enter_context(nc.semaphore(f"{name}{u}")) for u in range(U)]

        half = sb("half", [P, U, J * H2])
        one = sb("one", [P, U, J * P])
        one_t = sb("one_t", [P, U, J * P])
        hid = sb("hid", [P, U, J * D])
        weighted = sb("weighted", [P, U, J * D])
        loaded, rel_ready, one_ready, one_turned, one_t_ready = map(
            sems, ("half_loaded", "rel_ready", "one_ready", "one_turned", "one_t_ready"))
        summed, leaky, scaled, logit_ready = map(
            sems, ("hidden_summed", "leaky_ready", "hidden_scaled", "logit_ready"))
        flat = sems("hidden_copied")
        turn_ps = [t.psum[:, u, :] for u in range(U)]
        hid_ps = [t.psum[:, 2 + u, :] for u in range(U)]

        with nc.Block() as block:
            @block.sync
            def _(sp):
                def body(i):
                    for u in range(U):
                        wait_used(sp, summed[u], i)
                        load_tiles(nc, pl, t, sp, i, u, half, 0, H2, loaded)
                repeat(sp, N_IT, body)

            @block.tensor
            def _(pe):
                def body(i):
                    for u in range(U):
                        pe.wait_ge(one_ready[u], i + 1)
                        wait_used(pe, one_t_ready[u], i)
                        for j in range(J):
                            last = nc.tensor.transpose(turn_ps[u][:, j * P:(j + 1) * P],
                                                       one[:, u, j * P:(j + 1) * P], t.ident[:, :])
                        last.then_inc(one_turned[u], 1)
                    for u in range(U):
                        pe.wait_ge(one_t_ready[u], i + 1)
                        wait_used(pe, flat[u], i)
                        for j in range(J):
                            b = pe.value_load(t.tile_bucket[0:1, ds((i * U + u) * J + j, 1)],
                                              min_val=0, max_val=pl.NT - 1)
                            to = hid_ps[u][:, j * D:(j + 1) * D]
                            nc.tensor.matmul(to, one_t[:, u, j * P:(j + 1) * P],
                                             t.node_a[:, ds(b * D, D)], start=True, stop=False)
                            last = nc.tensor.matmul(to, t.ident[:, :], half[:, u, j * H2:j * H2 + D],
                                                    start=False, stop=True)
                        last.then_inc(summed[u], 1)
                repeat(pe, N_IT, body)

            @block.scalar
            def _(act):
                def body(i):
                    for u in range(U):
                        act.wait_ge(one_turned[u], i + 1)
                        wait_used(act, summed[u], i)
                        nc.scalar.copy(one_t[:, u, :], turn_ps[u]).then_inc(one_t_ready[u], 1)
                    for u in range(U):
                        act.wait_ge(summed[u], i + 1)
                        wait_used(act, leaky[u], i)
                        nc.scalar.copy(hid[:, u, :], hid_ps[u]).then_inc(flat[u], 1)
                repeat(act, N_IT, body)

            @block.vector
            def _(dve):
                v = nc.vector
                def body(i):
                    for u in range(U):
                        col = (i * U + u) * J
                        dve.wait_ge(loaded[u], i * (16 * J) + 16 * J)
                        v.tensor_tensor(t.rel[:, ds(col, J)], half[:, u, D:J * H2:H2],
                                        t.tile_base[:, ds(col, J)], ALU.subtract).then_inc(rel_ready[u], 1)
                        dve.wait_ge(rel_ready[u], i + 1)
                        wait_used(dve, one_turned[u], i)
                        v.tensor_tensor(one[:, u, :].rearrange("p (j n) -> p j n", j=J),
                                        over(t.rel[:, ds(col, J)], P), under(t.lane[:, :], J),
                                        ALU.is_equal).then_inc(one_ready[u], 1)
                    for u in range(U):
                        col = (i * U + u) * J
                        dve.wait_ge(flat[u], i + 1)
                        wait_used(dve, scaled[u], i)
                        v.scalar_tensor_tensor(hid[:, u, :], hid[:, u, :], SLOPE, hid[:, u, :],
                                               ALU.mult, ALU.max).then_inc(leaky[u], 1)
                        dve.wait_ge(leaky[u], i + 1)
                        v.tensor_tensor(weighted[:, u, :].rearrange("p (j f) -> p j f", j=J),
                                        hid[:, u, :].rearrange("p (j f) -> p j f", j=J),
                                        under(t.attn[:, :], J), ALU.mult).then_inc(scaled[u], 1)
                        dve.wait_ge(scaled[u], i + 1)
                        v.tensor_reduce(t.logits[:, ds(col * H, J * H)], weighted[:, u, :].rearrange(
                            "p (k d) -> p k d", d=HD), AX.X, ALU.add).then_inc(logit_ready[u], 1)
                repeat(dve, N_IT, body)


def maxima(nc, pl, t):
    H, ST = pl.H, pl.ST
    N_IT = ST // U
    with ExitStack() as ctx:
        def sb(name, shape, dt=F32):
            return ctx.enter_context(nc.sbuf_tensor(name, shape, dt))

        def sem(name):
            return ctx.enter_context(nc.semaphore(name))

        def sems(name):
            return [sem(f"{name}{u}") for u in range(U)]

        barred = sb("barred", [P, U, P])
        spread = sb("spread", [P, U, H * P])
        new_up = sb("new_up", [P, ST])
        new_down = sb("new_down", [P, ST])
        barred_ready, spread_ready, spread_turned, tile_done = map(
            sems, ("barred_ready", "spread_ready", "spread_turned", "tile_max_ready"))
        order = sem("max_order")
        turn_ps = [t.psum[:, 2 * u:2 * u + 2, :] for u in range(U)]
        HB = 512 // P

        with nc.Block() as block:
            @block.tensor
            def _(pe):
                def body(i):
                    for u in range(U):
                        pe.wait_ge(spread_ready[u], i + 1)
                        wait_used(pe, tile_done[u], i)
                        for h in range(H):
                            last = nc.tensor.transpose(
                                turn_ps[u][:, h // HB, (h % HB) * P:(h % HB + 1) * P],
                                spread[:, u, h * P:(h + 1) * P], t.ident[:, :])
                        last.then_inc(spread_turned[u], 1)
                repeat(pe, N_IT, body)

            @block.vector
            def _(dve):
                v = nc.vector
                def body(i):
                    for u in range(U):
                        tile = i * U + u
                        wait_used(dve, spread_ready[u], i)
                        v.tensor_scalar(barred[:, u, :], t.lane[:, :], t.rel[:, ds(tile, 1)], NEG,
                                        ALU.not_equal, ALU.mult).then_inc(barred_ready[u], 1)
                        dve.wait_ge(barred_ready[u], i + 1)
                        wait_used(dve, spread_turned[u], i)
                        v.tensor_tensor(spread[:, u, :].rearrange("p (h n) -> p h n", h=H),
                                        over(t.logits[:, ds(tile * H, H)], P),
                                        under(barred[:, u, :], H), ALU.add).then_inc(spread_ready[u], 1)
                    for u in range(U):
                        tile = i * U + u
                        dve.wait_ge(spread_turned[u], i + 1)
                        v.tensor_reduce(t.tile_max[:, :, ds(tile, 1)],
                                        turn_ps[u].rearrange("p b (k e) -> p (b k) e", e=P),
                                        AX.X, ALU.max).then_inc(tile_done[u], 1)
                repeat(dve, N_IT, body)
                for u in range(U):
                    dve.wait_ge(tile_done[u], N_IT)
                chain = Chain(dve, order)
                v.memset(new_up[:, 0:1], 0.0)
                v.memset(new_down[:, ST - 1:ST], 0.0)
                v.tensor_tensor(new_up[:, 1:ST], t.tile_base[:, 1:ST], t.tile_base[:, 0:ST - 1],
                                ALU.not_equal)
                chain.then(v.tensor_tensor(new_down[:, 0:ST - 1], t.tile_base[:, 1:ST],
                                           t.tile_base[:, 0:ST - 1], ALU.not_equal))
                v.tensor_scalar(new_up[:, :], new_up[:, :], NEG, None, ALU.mult)
                chain.then(v.tensor_scalar(new_down[:, :], new_down[:, :], NEG, None, ALU.mult))
                for h in range(H):
                    last = v.tensor_tensor_scan(t.node_max[:, h, :], new_up[:, :],
                                                t.tile_max[:, h, :], NEG, ALU.add, ALU.max)
                chain.then(last)
                for h in range(H):
                    last = (v.tensor_tensor_scan(t.tile_max[:, h, ::-1], new_down[:, ::-1],
                                                    t.tile_max[:, h, ::-1], NEG, ALU.add, ALU.max))
                chain.then(last)
                chain.then(v.tensor_tensor(t.node_max[:, :, :], t.node_max[:, :, :],
                                           t.tile_max[:, :, :], ALU.max))


def sums(nc, pl, t):
    D, H, HD, H2, WM = pl.D, pl.H, pl.HD, pl.HALF, pl.WM
    N_IT = pl.SG // U
    with ExitStack() as ctx:
        def sb(name, shape, dt=F32):
            return ctx.enter_context(nc.sbuf_tensor(name, shape, dt))

        def sem(name):
            return ctx.enter_context(nc.semaphore(name))

        def sems(name):
            return [sem(f"{name}{u}") for u in range(U)]

        msg = sb("msg", [P, U, J * D])
        one = sb("one_s", [P, U, J * P])
        one_t = sb("one_ts", [P, U, J * P])
        below = sb("below", [P, U, J * H])
        wm = sb("wm", [P, U, J * WM])
        loaded, one_ready, one_turned, one_t_ready, max_ready = map(
            sems, ("msg_loaded", "one_s_ready", "one_s_turned", "one_ts_ready", "edge_max_ready"))
        below_ready, capped, exp_ready, wm_ready, tile_summed = map(
            sems, ("below_ready", "capped", "exp_ready", "wm_ready", "tile_summed"))
        added = sem("added")
        turn_ps = [t.psum[:, u, :] for u in range(U)]
        max_ps = [t.psum[:, 2 + u, 0:J * H] for u in range(U)]
        sum_ps = [t.psum[:, 4 + 2 * u:6 + 2 * u, :] for u in range(U)]

        with nc.Block() as block:
            @block.sync
            def _(sp):
                def body(i):
                    for u in range(U):
                        wait_used(sp, wm_ready[u], i)
                        load_tiles(nc, pl, t, sp, i, u, msg, H2, D, loaded)
                repeat(sp, N_IT, body)

            @block.tensor
            def _(pe):
                def body(i):
                    for u in range(U):
                        pe.wait_ge(one_ready[u], i + 1)
                        wait_used(pe, one_t_ready[u], i)
                        for j in range(J):
                            last = nc.tensor.transpose(turn_ps[u][:, j * P:(j + 1) * P],
                                                       one[:, u, j * P:(j + 1) * P], t.ident[:, :])
                        last.then_inc(one_turned[u], 1)
                    for u in range(U):
                        pe.wait_ge(one_t_ready[u], i + 1)
                        wait_used(pe, below_ready[u], i)
                        for j in range(J):
                            tile = (i * U + u) * J + j
                            last = nc.tensor.matmul(max_ps[u][:, j * H:(j + 1) * H],
                                                    one_t[:, u, j * P:(j + 1) * P],
                                                    t.node_max[:, :, ds(tile, 1)],
                                                    start=True, stop=True)
                        last.then_inc(max_ready[u], 1)
                    for u in range(U):
                        pe.wait_ge(wm_ready[u], i + 1)
                        wait_used(pe, added, (i * U + u) * J)
                        for j in range(J):
                            last = nc.tensor.matmul(
                                sum_ps[u][:, j // 2, (j % 2) * WM:(j % 2 + 1) * WM],
                                one[:, u, j * P:(j + 1) * P], wm[:, u, j * WM:(j + 1) * WM],
                                start=True, stop=True)
                        last.then_inc(tile_summed[u], 1)
                repeat(pe, N_IT, body)

            @block.scalar
            def _(act):
                def body(i):
                    for u in range(U):
                        act.wait_ge(one_turned[u], i + 1)
                        wait_used(act, max_ready[u], i)
                        nc.scalar.copy(one_t[:, u, :], turn_ps[u]).then_inc(one_t_ready[u], 1)
                    for u in range(U):
                        act.wait_ge(capped[u], i + 1)
                        wait_used(act, tile_summed[u], i)
                        nc.scalar.activation(
                            wm[:, u, :].rearrange("p (j f) -> p j f", j=J)[:, :, D:WM],
                            below[:, u, :].rearrange("p (j h) -> p j h", j=J),
                            ACT.Exp).then_inc(exp_ready[u], 1)
                repeat(act, N_IT, body)

            @block.gpsimd
            def _(pool):
                def body(i):
                    for u in range(U):
                        pool.wait_ge(loaded[u], i * (16 * J) + 16 * J)
                        pool.wait_ge(exp_ready[u], i + 1)
                        for j in range(J):
                            last = nc.gpsimd.tensor_tensor(
                                wm[:, u, j * WM:j * WM + D].rearrange("p (h d) -> p h d", d=HD),
                                msg[:, u, j * D:(j + 1) * D].rearrange("p (h d) -> p h d", d=HD),
                                over(wm[:, u, j * WM + D:(j + 1) * WM], HD), ALU.mult)
                        last.then_inc(wm_ready[u], 1)
                repeat(pool, N_IT, body)

            @block.vector
            def _(dve):
                v = nc.vector
                v.memset(t.nodes_flat[:, :], 0.0).then_inc(added, J * (U - 1))
                def body(i):
                    for u in range(U):
                        col = (i * U + u) * J
                        wait_used(dve, tile_summed[u], i)
                        v.tensor_tensor(one[:, u, :].rearrange("p (j n) -> p j n", j=J),
                                        over(t.rel[:, ds(col, J)], P), under(t.lane[:, :], J),
                                        ALU.is_equal).then_inc(one_ready[u], 1)
                    for u in range(U):
                        col = (i * U + u) * J
                        dve.wait_ge(max_ready[u], i + 1)
                        wait_used(dve, exp_ready[u], i)
                        v.tensor_tensor(below[:, u, :], t.logits[:, ds(col * H, J * H)], max_ps[u],
                                        ALU.subtract).then_inc(below_ready[u], 1)
                        dve.wait_ge(below_ready[u], i + 1)
                        v.tensor_scalar(below[:, u, :], below[:, u, :], 0.0, None,
                                        ALU.min).then_inc(capped[u], 1)
                    for u in range(U):
                        dve.wait_ge(tile_summed[u], i + 1)
                        for j in range(J):
                            tile = (i * U + u) * J + j
                            b = dve.value_load(t.tile_bucket[0:1, ds(tile, 1)], min_val=0,
                                               max_val=pl.NT - 1)
                            acc = t.nodes_flat[:, ds(b * WM, WM)]
                            dve.wait_ge(added, tile + J * (U - 1))
                            last = v.tensor_tensor(acc, acc, sum_ps[u][:, j // 2, (j % 2) * WM:(j % 2 + 1) * WM],
                                                   ALU.add).then_inc(added, 1)
                repeat(dve, N_IT, body)


def output(nc, pl, t):
    D, H, HD, WM, NT = pl.D, pl.H, pl.HD, pl.WM, pl.NT
    N_IT = NT // U
    with ExitStack() as ctx:
        def sb(name, shape, dt=F32):
            return ctx.enter_context(nc.sbuf_tensor(name, shape, dt))

        def sem(name):
            return ctx.enter_context(nc.semaphore(name))

        def sems(name):
            return [sem(f"{name}{u}") for u in range(U)]

        inv = sb("inv", [P, NT, H])
        xs = sb("xs", [P, NT * D])
        mean = sb("mean", [P, U, D])
        mean_t = sb("mean_t", [P, U, D])
        x_loaded = sem("x_again")
        x_biased = sem("x_biased")
        order = sem("out_order")
        mean_ready, mean_turned, mean_t_ready, projected, out_ready = map(
            sems, ("mean_ready", "mean_turned", "mean_t_ready", "out_projected", "out_ready"))
        stored = sem("out_stored")
        turn_ps = [t.psum[:, u, 0:D] for u in range(U)]
        proj_ps = [t.psum[:, 2 + u, 0:D] for u in range(U)]
        xv = xs[:, :].rearrange("p (t f) -> p t f", f=D)

        with nc.Block() as block:
            @block.sync
            def _(sp):
                sp.dma_start(xv[:, 0:pl.WHOLE_N, :], t.x[0:pl.WHOLE_N * P, :].rearrange(
                    "(t p) f -> p t f", p=P)).then_inc(x_loaded, 16)
                sp.wait_ge(x_biased, 1)
                sp.dma_start(xv[0:pl.REST_N, pl.WHOLE_N, :],
                             t.x[pl.WHOLE_N * P:pl.N, :]).then_inc(x_loaded, 16)
                for u in range(U):
                    sp.wait_ge(out_ready[u], N_IT)
                sp.dma_start(t.out[0:pl.WHOLE_N * P, :].rearrange("(t p) f -> p t f", p=P),
                             xv[:, 0:pl.WHOLE_N, :]).then_inc(stored, 16)
                sp.dma_start(t.out[pl.WHOLE_N * P:pl.N, :],
                             xv[0:pl.REST_N, pl.WHOLE_N, :]).then_inc(stored, 16)
                sp.wait_ge(stored, 32)

            @block.tensor
            def _(pe):
                def body(i):
                    for u in range(U):
                        pe.wait_ge(mean_ready[u], i + 1)
                        wait_used(pe, mean_t_ready[u], i)
                        nc.tensor.transpose(turn_ps[u], mean[:, u, :], t.ident[:, :]).then_inc(mean_turned[u], 1)
                    for u in range(U):
                        pe.wait_ge(mean_t_ready[u], i + 1)
                        wait_used(pe, out_ready[u], i)
                        nc.tensor.matmul(proj_ps[u], mean_t[:, u, :], t.w_out[:, :],
                                         start=True, stop=True).then_inc(projected[u], 1)
                repeat(pe, N_IT, body)

            @block.scalar
            def _(act):
                def body(i):
                    for u in range(U):
                        act.wait_ge(mean_turned[u], i + 1)
                        wait_used(act, projected[u], i)
                        nc.scalar.copy(mean_t[:, u, :], turn_ps[u]).then_inc(mean_t_ready[u], 1)
                repeat(act, N_IT, body)

            @block.vector
            def _(dve):
                v = nc.vector
                chain = Chain(dve, order)
                v.memset(xv[:, pl.WHOLE_N:NT, :], 0.0).then_inc(x_biased, 1)
                chain.then(v.tensor_scalar(inv[:, :, :], t.nodes[:, :, D:WM], 1e-37, None, ALU.max))
                chain.then(v.reciprocal(inv[:, :, :], inv[:, :, :]))
                dve.wait_ge(x_loaded, 32)
                chain.then(v.tensor_tensor(xv[:, :, :], xv[:, :, :], under(t.out_bias[:, :], NT), ALU.add))
                inv_flat = inv[:, :, :].rearrange("p t h -> p (t h)")
                def body(i):
                    for u in range(U):
                        b = i * U + u
                        wait_used(dve, mean_turned[u], i)
                        v.tensor_tensor(mean[:, u, :].rearrange("p (h d) -> p h d", d=HD),
                                        t.nodes_flat[:, ds(b * WM, D)].rearrange("p (h d) -> p h d", d=HD),
                                        over(inv_flat[:, ds(b * H, H)], HD),
                                        ALU.mult).then_inc(mean_ready[u], 1)
                    for u in range(U):
                        b = i * U + u
                        dve.wait_ge(projected[u], i + 1)
                        v.tensor_tensor(xs[:, ds(b * D, D)], xs[:, ds(b * D, D)], proj_ps[u],
                                        ALU.add).then_inc(out_ready[u], 1)
                repeat(dve, N_IT, body)


def kernel(**inputs):
    import numpy as np
    from concourse import bacc
    from concourse.bass_utils import run_bass_kernel_spmd

    def arr(name):
        return np.asarray(inputs[name])

    D = arr("x").shape[1]
    msg_w = arr("L0_gnn_msg_w")
    arrays = {
        "x": arr("x"), "src": arr("src"), "dst": arr("dst"), "edge_attr": arr("edge_attr_128"),
        "w_node": np.concatenate([arr("L0_gnn_ni_w").T, arr("L0_gnn_nj_w").T, msg_w[:, :D].T], 1),
        "w_edge": np.concatenate([arr("L0_gnn_e_w").T, msg_w[:, D:].T], 1),
        "w_out": arr("L0_gnn_out_w").T,
        "ni_b": arr("L0_gnn_ni_b"), "nj_b": arr("L0_gnn_nj_b"), "e_b": arr("L0_gnn_e_b"),
        "msg_b": arr("L0_gnn_msg_b"), "out_b": arr("L0_gnn_out_b"),
        "attn": arr("L0_gnn_attn_proj").reshape(-1),
    }
    arrays = {k: np.ascontiguousarray(a) for k, a in arrays.items()}
    nc = bacc.Bacc("TRN2", target_bir_lowering=False, num_devices=1)
    aps = [nc.dram_tensor("in_" + k, a.shape, mybir.dt.from_np(a.dtype), kind="ExternalInput").ap()
           for k, a in arrays.items()]
    out = nc.dram_tensor("out", arrays["x"].shape, F32, kind="ExternalOutput").ap()
    gnn_kernel(nc, *aps, out)
    r = run_bass_kernel_spmd(nc, [{"in_" + k: a for k, a in arrays.items()}], core_ids=[0])
    return r.results[0]["out"]
```

```python
from contextlib import ExitStack

import concourse.bass as bass
from concourse import mybir
from concourse.alu_op_type import AluOpType as ALU

F32 = mybir.dt.float32
BF16 = mybir.dt.bfloat16
I32 = mybir.dt.int32
ACT = mybir.ActivationFunctionType
AX = mybir.AxisListType
ds = bass.ds

P = 128
J = 4
GROUP = P * J
K = 2
Q = J // K
U = 2
R = 4
SPAN = 60.0
NEG = -1.0e38
FAR = 1 << 20
LN_EPS = 1e-5
SLOPE = 0.2


class Plan:

    def __init__(self, n_nodes, n_edges, dim, heads):
        self.N, self.E, self.D, self.H = n_nodes, n_edges, dim, heads
        self.HD = dim // heads
        self.NT = -(-n_nodes // (P * U)) * U
        self.WHOLE_N = n_nodes // P
        self.REST_N = n_nodes - self.WHOLE_N * P
        full = -(-n_edges // GROUP)
        self.EG = -(-full // R) * R
        self.WHOLE = n_edges // GROUP
        self.REST = n_edges - self.WHOLE * GROUP
        self.EC = self.EG * J
        units = n_edges // (P * K) + self.NT
        self.SG = -(-units // (Q * R)) * R
        self.SU = self.SG * Q
        self.ST = self.SG * J
        self.HALF = dim + 4
        self.ROW = 2 * self.HALF
        self.WM = dim + heads


class Tensors:

    def __init__(self, nc):
        self.nc, self.taken = nc, []

    def semaphore(self, name):
        self.taken.append(self.nc.alloc_semaphore(name))
        return self.taken[-1]

    def meet(self):
        self.nc.clear_and_free_semaphores(self.taken)
        self.nc.all_engine_barrier()
        self.taken = []


class Chain:

    def __init__(self, engine, sem):
        self.engine, self.sem, self.n = engine, sem, 0

    def then(self, instruction):
        self.n += 1
        instruction.then_inc(self.sem, 1)
        self.engine.wait_ge(self.sem, self.n)


def gnn_kernel(nc, x, src, dst, edge_attr, w_node, w_edge, w_out, ni_b, nj_b, e_b, msg_b, out_b,
               attn, out):
    N, D = x.shape
    E = src.shape[0]
    H = 8
    pl = Plan(N, E, D, H)
    with ExitStack() as whole:
        def sb(name, shape, dt=F32):
            return whole.enter_context(nc.sbuf_tensor(name, shape, dt))

        t = Tensors(nc)
        t.x, t.src, t.dst, t.edge_attr, t.out = x, src, dst, edge_attr, out
        t.w_node_d, t.w_edge_d, t.w_out_d, t.attn_d, t.out_b_d = w_node, w_edge, w_out, attn, out_b
        t.ni_b, t.nj_b, t.e_b, t.msg_b = ni_b, nj_b, e_b, msg_b
        t.bm = nc.dram_tensor("dst_table", [pl.NT * P, 2 * D], F32).ap()
        t.rows = nc.dram_tensor("sorted_rows", [E + K * P, pl.ROW], F32).ap()
        t.unit_bucket_d = nc.dram_tensor("unit_bucket_d", [-(-pl.SU // P) * P], I32).ap()
        t.unit_row_d = nc.dram_tensor("unit_row_d", [-(-pl.SU // P) * P], I32).ap()
        t.unit_base_d = nc.dram_tensor("unit_base_d", [-(-pl.SU // P) * P], F32).ap()
        t.psum = whole.enter_context(nc.psum_tensor("psum", [P, 8, 512], F32))
        t.node_a = sb("node_a", [P, pl.NT * D])
        t.nodes_flat = sb("nodes", [P, pl.NT * pl.WM])
        t.nodes = t.nodes_flat[:, :].rearrange("p (t f) -> p t f", t=pl.NT)
        t.shared = sb("shared", [P, 3 * pl.ST * H])
        t.hot = t.shared[:, 0:pl.EC * pl.NT // 2].bitcast(BF16).rearrange(
            "p (c b) -> p c b", b=pl.NT)
        t.logits = t.shared[:, 0:pl.ST * H]
        t.tile_max = t.shared[:, pl.ST * H:2 * pl.ST * H].rearrange("p (h t) -> p h t", h=H)
        t.node_max = t.shared[:, 2 * pl.ST * H:3 * pl.ST * H].rearrange("p (h t) -> p h t", h=H)
        t.below = t.shared[:, pl.ST * H:2 * pl.ST * H]
        t.masked = t.shared[:, 2 * pl.ST * H:3 * pl.ST * H]
        t.ident = sb("ident", [P, P])
        t.ones = sb("ones", [P, P])
        t.ones_bf = sb("ones_bf", [P, P], BF16)
        t.ident_bf = sb("ident_bf", [P, P], BF16)
        t.lane_bf = sb("lane_bf", [P, P], BF16)
        t.before_bf = sb("before_bf", [P, P], BF16)
        t.lane = sb("lane", [P, P])
        t.id1 = sb("id1", [P, pl.EC])
        t.pad_off = sb("pad_off", [P, pl.EC])
        t.dst_i = sb("dst_i", [P, pl.EC + U * J], I32)
        t.dst_rel = sb("dst_rel", [P, pl.EC], BF16)
        t.window_base = sb("window_base", [1, pl.EG], I32)
        t.near = sb("near", [1, 1], I32)
        t.start = sb("start", [P, pl.NT])
        t.tile_base = sb("tile_base", [P, pl.ST])
        t.unit_bucket = sb("unit_bucket", [1, pl.SU], I32)
        t.unit_row = sb("unit_row", [1, pl.SU], I32)
        t.rel = sb("rel", [P, pl.ST])
        t.top = sb("top", [P, H])
        t.wide = sb("wide", [1, 1], I32)
        t.w_edge = sb("w_edge", [P, 2 * D])
        t.w_out = sb("w_out", [P, D])
        t.attn = sb("attn", [P, D])
        t.out_bias = sb("out_bias", [P, D])
        tables(nc, pl, t)
        t.meet()
        buckets(nc, pl, t)
        t.meet()
        edges(nc, pl, t)
        t.meet()
        logits(nc, pl, t)
        t.meet()
        spread_of_logits(nc, pl, t)
        t.meet()
        maxima(nc, pl, t)
        t.meet()
        sums(nc, pl, t)
        t.meet()
        output(nc, pl, t)
        t.meet()


def repeat(engine, n, body):
    body(0)
    with engine.Fori(1, n) as i:
        body(i)


def wait_used(engine, semaphore, value):
    if not (isinstance(value, int) and value == 0):
        engine.wait_ge(semaphore, value)


def staggered(engine, n, steps, R=R):
    def body(i, opening):
        for u in range(R):
            for lag, step in steps:
                if u >= lag:
                    step(i, u - lag)
                elif not opening:
                    step(i - 1, u - lag + R)

    body(0, True)
    body(1, False)
    with engine.Fori(2, n) as i:
        body(i, False)
    for u in range(R):
        for lag, step in steps:
            if u < lag:
                step(n - 1, u - lag + R)


def held(engine, register, i, k):
    if isinstance(i, int):
        return i + k
    engine.reg_add(register, i, k)
    return engine.snap(register)


def over(ap, n):
    return ap.unsqueeze(2).to_broadcast([ap.shape[0], ap.shape[1], n])


def under(ap, n):
    return ap.unsqueeze(1).to_broadcast([ap.shape[0], n, ap.shape[1]])


def tables(nc, pl, t):
    D, NT = pl.D, pl.NT
    META = pl.EG // 2
    with ExitStack() as ctx:
        def sb(name, shape, dt=F32):
            return ctx.enter_context(nc.sbuf_tensor(name, shape, dt))

        def sem(name):
            return t.semaphore(name)

        w_node = sb("w_node", [P, 3 * D])
        bias = sb("bias", [P, 3 * D])
        bias_in = sb("bias_in", [P, 2, D])
        stats = sb("stats", [P, U, 6])
        moments = sb("moments", [P, U, 2])
        mean_var = sb("mean_var", [P, NT * 2])
        std = sb("std", [P, NT])
        rstd = sb("rstd", [P, NT])
        eps = sb("eps", [P, 1])
        normed = sb("normed", [P, U, D])
        h_t = sb("h_t", [P, U, D])
        bm_out = sb("bm_out", [P, U, 2 * D])
        meta_i = sb("meta_i", [META, 2, 2, GROUP], I32)
        meta_f = sb("meta_f", [META, 2, 2, GROUP])
        src_f = sb("src_f", [P, pl.EC])
        src_i = sb("src_i", [P, pl.EC], I32)
        hi_i = sb("hi_i", [P, pl.EC], I32)
        hi_bf = sb("hi_bf", [P, pl.EC], BF16)
        zero_row = sb("zero_row", [P, K * pl.ROW])

        cleared = sem("cleared")
        x_loaded = sem("x_loaded")
        meta_loaded = sem("meta_loaded")
        weights_loaded = sem("weights_loaded")
        bias_loaded = sem("bias_loaded")
        consts_ready = sem("consts_ready")
        pool_chain = sem("pool_chain")
        dve_chain = sem("dve_chain")
        stats_ready = [sem(f"stats_ready{u}") for u in range(U)]
        moments_ready = [sem(f"moments_ready{u}") for u in range(U)]
        var_ready = [sem(f"var_ready{u}") for u in range(U)]
        std_ready = sem("std_ready")
        rstd_ready = sem("rstd_ready")
        bias_ready = sem("bias_ready")
        meta_cast = sem("meta_cast")
        meta_turned = sem("meta_turned")
        meta_copied = sem("meta_copied")
        normed_ready = [sem(f"normed_ready{u}") for u in range(U)]
        turned = [sem(f"turned{u}") for u in range(U)]
        h_ready = [sem(f"h_ready{u}") for u in range(U)]
        projected = [sem(f"projected{u}") for u in range(U)]
        bm_ready = [sem(f"bm_ready{u}") for u in range(U)]
        bm_stored = [sem(f"bm_stored{u}") for u in range(U)]
        slack_stored = sem("slack_stored")
        xs = t.nodes[:, :, 0:D]
        turn_ps = [t.psum[:, u, 0:D] for u in range(U)]
        proj_ps = [t.psum[:, 2 + u, 0:3 * D] for u in range(U)]
        meta_ps = [t.psum[:, 4 + k, 0:J * META].rearrange("p (j g) -> p j g", j=J)
                   for k in range(4)]

        with nc.Block() as block:
            @block.sync
            def _(sp):
                sp.wait_ge(cleared, 4)
                whole0 = min(META, pl.WHOLE)
                whole1 = pl.WHOLE - whole0
                for k, ids in enumerate((t.src, t.dst)):
                    sp.dma_start(meta_i[0:whole0, k, 0, :], ids[0:whole0 * GROUP].rearrange(
                        "(g c) -> g c", c=GROUP)).then_inc(meta_loaded, 16)
                    sp.dma_start(meta_i[0:whole1, k, 1, :],
                                 ids[whole0 * GROUP:pl.WHOLE * GROUP].rearrange(
                                     "(g c) -> g c", c=GROUP)).then_inc(meta_loaded, 16)
                    sp.dma_start(meta_i[whole1:whole1 + 1, k, 1, 0:pl.REST],
                                 ids[pl.WHOLE * GROUP:pl.E].rearrange(
                                     "(g c) -> g c", g=1)).then_inc(meta_loaded, 16)
                sp.dma_start(xs[:, 0:pl.WHOLE_N, :], t.x[0:pl.WHOLE_N * P, :].rearrange(
                    "(t p) f -> p t f", p=P)).then_inc(x_loaded, 16)
                sp.dma_start(xs[0:pl.REST_N, pl.WHOLE_N, :],
                             t.x[pl.WHOLE_N * P:pl.N, :]).then_inc(x_loaded, 16)
                sp.dma_start(t.rows[pl.E:pl.E + K * P, :].rearrange("(p k) f -> p (k f)", k=K),
                             zero_row[:, :]).then_inc(slack_stored, 16)
                def body(i):
                    for u in range(U):
                        sp.wait_ge(bm_ready[u], i + 1)
                        sp.dma_start(t.bm[ds((i * U + u) * P, P), :],
                                     bm_out[:, u, :]).then_inc(bm_stored[u], 16)
                repeat(sp, NT // U, body)
                for u in range(U):
                    sp.wait_ge(bm_stored[u], 16 * (NT // U))
                sp.wait_ge(slack_stored, 16)

            @block.gpsimd
            def _(pool):
                chain = Chain(pool, pool_chain)
                nc.gpsimd.memset(meta_i[:, 0, :, :], NT * P).then_inc(cleared, 1)
                nc.gpsimd.memset(meta_i[:, 1, :, :], 0).then_inc(cleared, 1)
                nc.gpsimd.memset(xs[:, pl.WHOLE_N:NT, :], 0.0).then_inc(cleared, 1)
                nc.gpsimd.memset(zero_row[:, :], 0.0).then_inc(cleared, 1)
                chain.then(nc.gpsimd.memset(t.ones[:, :], 1.0))
                nc.gpsimd.memset(t.ones_bf[:, :], 1.0)
                nc.gpsimd.iota(t.lane[:, :], [[1, P]], base=0, channel_multiplier=0,
                               allow_small_or_imprecise_dtypes=True)
                nc.gpsimd.iota(t.lane_bf[:, :], [[1, P]], base=0, channel_multiplier=0,
                               allow_small_or_imprecise_dtypes=True)
                nc.gpsimd.affine_select(out=t.ident[:, :], in_=t.ones[:, :], pattern=[[1, P]],
                                        compare_op=ALU.is_equal, fill=0.0, base=0,
                                        channel_multiplier=-1)
                nc.gpsimd.affine_select(out=t.ident_bf[:, :], in_=t.ones[:, :], pattern=[[1, P]],
                                        compare_op=ALU.is_equal, fill=0.0, base=0,
                                        channel_multiplier=-1)
                nc.gpsimd.affine_select(out=t.before_bf[:, :], in_=t.ones[:, :],
                                        pattern=[[1, P]], compare_op=ALU.is_gt, fill=0.0, base=0,
                                        channel_multiplier=-1).then_inc(consts_ready, 1)

            @block.scalar
            def _(act):
                act.dma_start(w_node[:, :], t.w_node_d).then_inc(weights_loaded, 16)
                act.dma_start(t.w_edge[:, :], t.w_edge_d).then_inc(weights_loaded, 16)
                act.dma_start(t.w_out[:, :], t.w_out_d).then_inc(weights_loaded, 16)
                act.dma_start(t.attn[:, :], t.attn_d.partition_broadcast(P)).then_inc(weights_loaded, 16)
                act.dma_start(t.out_bias[:, :], t.out_b_d.partition_broadcast(P)).then_inc(weights_loaded, 16)
                act.dma_start(bias[:, 0:D], t.ni_b.partition_broadcast(P)).then_inc(bias_loaded, 16)
                act.dma_start(bias[:, 2 * D:3 * D], t.msg_b.partition_broadcast(P)).then_inc(bias_loaded, 16)
                act.dma_start(bias_in[:, 0, :], t.nj_b.partition_broadcast(P)).then_inc(bias_loaded, 16)
                act.dma_start(bias_in[:, 1, :], t.e_b.partition_broadcast(P)).then_inc(bias_loaded, 16)
                for u in range(U):
                    act.wait_ge(var_ready[u], NT // U)
                nc.scalar.activation(std[:, :], mean_var[:, 1:2 * NT:2], ACT.Sqrt,
                                     bias=eps[:, :]).then_inc(std_ready, 1)
                def body(i):
                    for u in range(U):
                        act.wait_ge(turned[u], i + 1)
                        wait_used(act, projected[u], i)
                        nc.scalar.activation(h_t[:, u, :], turn_ps[u],
                                             ACT.Relu).then_inc(h_ready[u], 1)
                repeat(act, NT // U, body)
                act.wait_ge(weights_loaded, 16 * 5)

            @block.tensor
            def _(pe):
                pe.wait_ge(consts_ready, 1)
                pe.wait_ge(meta_cast, 1)
                for k in range(2):
                    for half in range(2):
                        for j in range(J):
                            last = nc.tensor.transpose(meta_ps[2 * k + half][:, j, :],
                                                       meta_f[:, k, half, j:GROUP:J],
                                                       t.ident[0:META, 0:META])
                        last.then_inc(meta_turned, 1)
                pe.wait_ge(weights_loaded, 16 * 5)

                def body(i):
                    for u in range(U):
                        pe.wait_ge(normed_ready[u], i + 1)
                        wait_used(pe, h_ready[u], i)
                        nc.tensor.transpose(turn_ps[u], normed[:, u, :],
                                            t.ident[:, :]).then_inc(turned[u], 1)
                    for u in range(U):
                        pe.wait_ge(h_ready[u], i + 1)
                        wait_used(pe, bm_ready[u], i)
                        nc.tensor.matmul(proj_ps[u], h_t[:, u, :], w_node[:, :],
                                         start=True, stop=True).then_inc(projected[u], 1)
                repeat(pe, NT // U, body)

            @block.vector
            def _(dve):
                chain = Chain(dve, dve_chain)
                nc.vector.memset(eps[:, :], LN_EPS)
                chain.then(nc.vector.memset(t.dst_i[:, :], 0))
                dve.wait_ge(meta_loaded, 16 * 6)
                nc.vector.tensor_copy(meta_f[:, :, :, :].rearrange("g k h c -> g (k h c)"),
                                      meta_i[:, :, :, :].rearrange("g k h c -> g (k h c)")).then_inc(meta_cast, 1)
                dve.wait_ge(x_loaded, 32)
                reg = dve.alloc_register("after")
                def body(i):
                    after = held(dve, reg, i, 1)
                    for u in range(U):
                        wait_used(dve, moments_ready[u], i)
                        nc.vector.bn_stats(stats[:, u, :], t.nodes_flat[:, ds((i * U + u) * pl.WM, D)]
                                           ).then_inc(stats_ready[u], 1)
                    for u in range(U):
                        dve.wait_ge(x_loaded, 32)
                        dve.wait_ge(stats_ready[u], after)
                        wait_used(dve, var_ready[u], i)
                        nc.vector.bn_aggr(moments[:, u, :], stats[:, u, :]).then_inc(moments_ready[u], 1)
                    for u in range(U):
                        dve.wait_ge(moments_ready[u], i + 1)
                        nc.vector.tensor_copy(mean_var[:, ds((i * U + u) * 2, 2)],
                                              moments[:, u, :]).then_inc(var_ready[u], 1)
                repeat(dve, NT // U, body)
                for k in range(2):
                    for half in range(2):
                        dve.wait_ge(meta_turned, 2 * k + half + 1)
                        to = (src_f if k == 0 else t.dst_i)[:, 0:pl.EC].rearrange(
                            "p (g j) -> p j g", j=J)[:, :, half * META:(half + 1) * META]
                        last = nc.vector.tensor_copy(to, meta_ps[2 * k + half])
                chain.then(last)
                nc.vector.tensor_scalar(t.id1[:, :], src_f[:, :], 1.0, None, ALU.add)
                nc.vector.tensor_scalar(t.pad_off[:, :], src_f[:, :], float(NT * P), float(FAR),
                                        ALU.is_ge, ALU.mult)
                chain.then(nc.vector.tensor_copy(src_i[:, :], src_f[:, :]))
                chain.then(nc.vector.tensor_scalar(hi_i[:, :], src_i[:, :], 7, None,
                                                   ALU.arith_shift_right))
                chain.then(nc.vector.tensor_copy(hi_bf[:, :], hi_i[:, :]))
                dve.wait_ge(bias_loaded, 16 * 4)
                chain.then(nc.vector.tensor_tensor(bias[:, 0:D], bias[:, 0:D], bias_in[:, 0, :], ALU.add))
                chain.then(nc.vector.tensor_tensor(bias[:, 0:D], bias[:, 0:D], bias_in[:, 1, :], ALU.add))
                chain.then(nc.vector.memset(bias[:, D:2 * D], 0.0))
                dve.wait_ge(std_ready, 1)
                chain.then(nc.vector.reciprocal(rstd[:, :], std[:, :]))

                def body(i):
                    for u in range(U):
                        it = i * U + u
                        wait_used(dve, turned[u], i)
                        nc.vector.tensor_scalar(normed[:, u, :], t.nodes_flat[:, ds(it * pl.WM, D)],
                                                mean_var[:, ds(it * 2, 1)], rstd[:, ds(it, 1)],
                                                ALU.subtract, ALU.mult).then_inc(normed_ready[u], 1)
                    for u in range(U):
                        it = i * U + u
                        dve.wait_ge(projected[u], i + 1)
                        wait_used(dve, bm_stored[u], i * 16)
                        nc.vector.tensor_tensor(t.node_a[:, ds(it * D, D)], proj_ps[u][:, 0:D],
                                                bias[:, 0:D], ALU.add)
                        nc.vector.tensor_tensor(bm_out[:, u, :], proj_ps[u][:, D:3 * D],
                                                bias[:, D:3 * D], ALU.add).then_inc(bm_ready[u], 1)
                repeat(dve, NT // U, body)
                dve.wait_ge(consts_ready, 1)
                step = pl.EC // 8
                for c in range(0, pl.EC, step):
                    nc.vector.tensor_tensor(t.hot[:, c:c + step, :],
                                            over(hi_bf[:, c:c + step], NT),
                                            under(t.lane_bf[:, 0:NT], step), ALU.is_equal)


def buckets(nc, pl, t):
    NT, SU = pl.NT, pl.SU
    C = -(-pl.SU // P)
    CH = 8
    with ExitStack() as ctx:
        def sb(name, shape, dt=F32):
            return ctx.enter_context(nc.sbuf_tensor(name, shape, dt))

        def sem(name):
            return t.semaphore(name)

        count = sb("count", [P, NT])
        units_i = sb("units_i", [P, NT], I32)
        units = sb("units", [P, NT])
        ends = sb("ends", [P, NT])
        unit_start = sb("unit_start", [P, NT])
        unit_id = sb("unit_id", [P, C])
        pairs = sb("pairs", [P, C, NT])
        chosen = sb("chosen", [P, C, NT])
        bucket = sb("bucket", [P, C])
        first_unit = sb("first_unit", [P, C])
        first_row = sb("first_row", [P, C])
        row = sb("row", [P, C])
        row_i = sb("row_i", [P, C], I32)
        bucket_i = sb("bucket_i", [P, C], I32)
        base = sb("base", [P, C])
        unit_base = sb("unit_base", [P, SU])
        EG, META = pl.EG, pl.EG // 2
        dst_f = sb("dst_f", [P, pl.EC])
        ends_of = sb("ends_of", [P, 2, EG])
        padded = sb("padded", [P, 2, pl.EC])
        per_group = sb("per_group", [META, 2, 2])
        group_row = sb("group_row", [1, 2, EG])
        most = sb("most", [1, 1])
        ends_ready = sem("dst_ends_ready")
        ends_turned = sem("dst_ends_turned")
        group_ready = sem("dst_group_ready")
        group_turned = sem("dst_group_turned")
        row_ready = sem("dst_row_ready")
        base_spread = sem("dst_base_spread")
        ends_ps = t.psum[0:META, 1, :]
        row_ps = t.psum[0:1, 2, 0:2 * EG]
        base_ps = t.psum[:, 3, 0:EG]
        counted = sem("counted")
        ids_ready = sem("ids_ready")
        order = sem("bucket_order")
        found = sem("units_found")
        stored = sem("units_stored")
        loaded = sem("units_loaded")
        hist = t.psum[:, 0, 0:CH * NT]

        with nc.Block() as block:
            @block.tensor
            def _(pe):
                rhs = t.hot[:, :, :].rearrange("p c b -> p (c b)")
                n = pl.EC // CH
                nc.tensor.matmul(hist, t.ones_bf[:, :], rhs[:, 0:CH * NT], start=True, stop=False)
                with pe.Fori(1, n - 1) as i:
                    nc.tensor.matmul(hist, t.ones_bf[:, :], rhs[:, ds(i * (CH * NT), CH * NT)],
                                     start=False, stop=False)
                nc.tensor.matmul(hist, t.ones_bf[:, :], rhs[:, (n - 1) * CH * NT:n * CH * NT],
                                 start=False, stop=True).then_inc(counted, 1)
                pe.wait_ge(ends_ready, 1)
                for k in range(2):
                    for half in range(2):
                        last = nc.tensor.transpose(
                            ends_ps[:, (2 * k + half) * P:(2 * k + half + 1) * P],
                            ends_of[:, k, half * META:(half + 1) * META], t.ident[:, :])
                last.then_inc(ends_turned, 1)
                pe.wait_ge(group_ready, 1)
                for k in range(2):
                    for half in range(2):
                        last = nc.tensor.transpose(
                            row_ps[:, (2 * k + half) * META:(2 * k + half + 1) * META],
                            per_group[:, k, half:half + 1], t.ident[0:META, 0:META])
                last.then_inc(group_turned, 1)
                pe.wait_ge(row_ready, 1)
                nc.tensor.matmul(base_ps, t.ones[0:1, :], group_row[:, 0, :],
                                 start=True, stop=True).then_inc(base_spread, 1)

            @block.gpsimd
            def _(pool):
                nc.gpsimd.iota(unit_id[:, :], [[P, C]], base=0, channel_multiplier=1,
                               allow_small_or_imprecise_dtypes=True).then_inc(ids_ready, 1)

            @block.vector
            def _(dve):
                chain = Chain(dve, order)
                v = nc.vector
                chain.then(v.tensor_copy(dst_f[:, :], t.dst_i[:, 0:pl.EC]))
                v.tensor_tensor(padded[:, 0, :], dst_f[:, :], t.pad_off[:, :], ALU.add)
                chain.then(v.tensor_tensor(padded[:, 1, :], dst_f[:, :], t.pad_off[:, :],
                                           ALU.subtract))
                v.tensor_reduce(ends_of[:, 0, :], padded[:, 0, :].rearrange(
                    "p (g j) -> p g j", j=J), AX.X, ALU.min)
                chain.then(v.tensor_reduce(ends_of[:, 1, :], padded[:, 1, :].rearrange(
                    "p (g j) -> p g j", j=J), AX.X, ALU.max))
                v.tensor_copy(most[:, :], ends_of[0:1, 0, 0:1]).then_inc(ends_ready, 1)
                dve.wait_ge(ends_turned, 1)
                v.tensor_reduce(per_group[:, 0, :], ends_ps[:, 0:2 * P].rearrange(
                    "g (h e) -> g h e", e=P), AX.X, ALU.min)
                chain.then(v.tensor_reduce(per_group[:, 1, :], ends_ps[:, 2 * P:4 * P].rearrange(
                    "g (h e) -> g h e", e=P), AX.X, ALU.max))
                chain.then(v.tensor_scalar(per_group[:, 0, :], per_group[:, 0, :],
                                           float((NT - 1) * P), None, ALU.min))
                v.tensor_tensor(per_group[:, 1, :], per_group[:, 1, :], per_group[:, 0, :],
                                ALU.subtract).then_inc(group_ready, 1)
                dve.wait_ge(group_turned, 1)
                v.tensor_copy(t.window_base[:, :], row_ps[:, 0:EG])
                v.tensor_copy(group_row[:, :, :].rearrange("a k g -> a (k g)"),
                              row_ps).then_inc(row_ready, 1)
                dve.wait_ge(row_ready, 1)
                chain.then(v.tensor_reduce(most[:, :], group_row[:, 1, :], AX.X, ALU.max))
                v.tensor_scalar(t.near[:, :], most[:, :], float(P) - 0.5, None, ALU.is_lt)
                dve.wait_ge(base_spread, 1)
                v.tensor_tensor(t.dst_rel[:, :].rearrange("p (g j) -> p g j", j=J),
                                dst_f[:, :].rearrange("p (g j) -> p g j", j=J),
                                over(base_ps, J), ALU.subtract)
                dve.wait_ge(counted, 1)
                chain.then(v.tensor_reduce(count[:, :], hist.rearrange("p (c b) -> p b c", c=CH),
                                           AX.X, ALU.add))
                chain.then(v.tensor_scalar(units[:, :], count[:, :], float(P * K - 1), None, ALU.add))
                chain.then(v.tensor_copy(units_i[:, :], units[:, :]))
                chain.then(v.tensor_scalar(units_i[:, :], units_i[:, :], (P * K).bit_length() - 1, None, ALU.arith_shift_right))
                chain.then(v.tensor_copy(units[:, :], units_i[:, :]))
                chain.then(v.tensor_tensor_scan(ends[:, :], t.ones[:, 0:NT], count[:, :], 0.0,
                                                ALU.mult, ALU.add))
                chain.then(v.tensor_tensor(t.start[:, :], ends[:, :], count[:, :], ALU.subtract))
                chain.then(v.tensor_tensor_scan(ends[:, :], t.ones[:, 0:NT], units[:, :], 0.0,
                                                ALU.mult, ALU.add))
                chain.then(v.tensor_tensor(unit_start[:, :], ends[:, :], units[:, :], ALU.subtract))
                dve.wait_ge(ids_ready, 1)
                chain.then(v.tensor_tensor(pairs[:, :, :], over(unit_id[:, :], NT),
                                           under(unit_start[:, :], C), ALU.is_ge))
                chain.then(v.tensor_reduce(bucket[:, :], pairs[:, :, :], AX.X, ALU.add))
                chain.then(v.tensor_scalar(bucket[:, :], bucket[:, :], -1.0, None, ALU.add))
                chain.then(v.tensor_tensor(pairs[:, :, :], over(bucket[:, :], NT),
                                           under(t.lane[:, 0:NT], C), ALU.is_equal))
                chain.then(v.tensor_tensor(chosen[:, :, :], pairs[:, :, :],
                                           under(unit_start[:, :], C), ALU.mult))
                chain.then(v.tensor_reduce(first_unit[:, :], chosen[:, :, :], AX.X, ALU.add))
                chain.then(v.tensor_tensor(chosen[:, :, :], pairs[:, :, :],
                                           under(t.start[:, :], C), ALU.mult))
                chain.then(v.tensor_reduce(first_row[:, :], chosen[:, :, :], AX.X, ALU.add))
                chain.then(v.tensor_tensor(row[:, :], unit_id[:, :], first_unit[:, :], ALU.subtract))
                chain.then(v.scalar_tensor_tensor(row[:, :], row[:, :], float(P * K), first_row[:, :],
                                                  ALU.mult, ALU.add))
                chain.then(v.tensor_scalar(row[:, :], row[:, :], float(pl.E), None, ALU.min))
                chain.then(v.tensor_copy(row_i[:, :], row[:, :]))
                chain.then(v.tensor_copy(bucket_i[:, :], bucket[:, :]))
                chain.then(v.tensor_scalar(base[:, :], bucket[:, :], float(P), 1.0, ALU.mult, ALU.add))
                v.tensor_copy(base[:, :], base[:, :]).then_inc(found, 1)
                dve.wait_ge(loaded, 48)
                v.tensor_copy(t.tile_base[:, :].rearrange("p (s k) -> p s k", k=K),
                              over(unit_base[:, :], K))

            @block.sync
            def _(sp):
                sp.wait_ge(found, 1)
                with nc.allow_non_contiguous_dma("a few hundred numbers"):
                    for to, of in ((t.unit_row_d, row_i), (t.unit_bucket_d, bucket_i),
                                   (t.unit_base_d, base)):
                        sp.dma_start(to.rearrange("(c p) -> p c", p=P), of[:, :]).then_inc(stored, 16)
                sp.wait_ge(stored, 48)
                sp.dma_start(t.unit_row[:, :], t.unit_row_d[0:SU].rearrange(
                    "(a n) -> a n", a=1)).then_inc(loaded, 16)
                sp.dma_start(t.unit_bucket[:, :], t.unit_bucket_d[0:SU].rearrange(
                    "(a n) -> a n", a=1)).then_inc(loaded, 16)
                sp.dma_start(unit_base[:, :], t.unit_base_d[0:SU].partition_broadcast(P)).then_inc(loaded, 16)
                sp.wait_ge(loaded, 48)


def edges(nc, pl, t):
    D, NT, H2 = pl.D, pl.NT, pl.HALF
    N_IT = pl.EG // U
    JN = J * NT
    with ExitStack() as ctx:
        def sb(name, shape, dt=F32):
            return ctx.enter_context(nc.sbuf_tensor(name, shape, dt))

        def sem(name):
            return t.semaphore(name)

        def sems(name):
            return [sem(f"{name}{u}") for u in range(U)]

        feat = sb("feat", [P, U, J * D])
        feat_t = sb("feat_t", [P, U, J * P])
        window = sb("window", [P, U, 2 * D])
        dst_hot = sb("dst_hot", [P, U, J * P], BF16)
        dst_hot_t = sb("dst_hot_t", [P, U, J * P])
        got = sb("got", [P, U, J * 2 * D])
        rows = sb("rows", [P, U, J * pl.ROW])
        dst_now = sb("dst_now", [P, U, J], I32)
        place = sb("place", [P, U, J], I32)
        place_f = sb("place_f", [P, U, J])
        rank = sb("rank", [P, U, JN])
        group_hot = sb("group_hot", [P, U, NT])
        before = sb("before", [P, U, NT])
        feat_loaded, turned, turned_copied, multiplied = map(
            sems, ("feat_loaded", "feat_turned", "feat_t_ready", "product_ready"))
        window_loaded, dst_hot_ready, dst_hot_turned, dst_hot_copied = map(
            sems, ("window_loaded", "dst_hot_ready", "dst_hot_turned", "dst_hot_t_ready"))
        gathered, dst_ready, ranked, picked, place_sum, place_ready, ids_ready = map(
            sems, ("gathered", "dst_ready", "ranked", "picked", "place_sum", "place_ready",
                   "ids_ready"))
        hot_summed, before_ready, rows_ready, scattered = map(
            sems, ("hot_summed", "before_ready", "rows_ready", "scattered"))
        rows_cleared = sem("rows_cleared")
        turn_ps = [t.psum[:, u, :] for u in range(U)]
        prod_ps = [t.psum[:, 2 + 2 * u:4 + 2 * u, :] for u in range(U)]
        rank_ps = t.psum[:, 6, 0:JN]
        hot_ps = t.psum[:, 7, 0:J * P // 2].bitcast(BF16)
        hot = t.hot.rearrange("p c b -> p (c b)")
        feat_d = t.edge_attr[0:pl.WHOLE * GROUP, :].rearrange("(g p j) f -> g p (j f)", p=P, j=J)
        rest_p = pl.REST // J

        def rows_view(u):
            return rows[:, u, :].rearrange("p (k f) -> p k f", f=H2)[:, :, 0:D]

        def prod_view(u):
            return prod_ps[u].rearrange("p b (k f) -> p (b k) f", f=D)

        def wait_last_group(engine, semaphores, i, u):
            wait_used(engine, semaphores[(u - 1) % U], i + 1 if u else i)

        def by_kind(engine, program):
            near = engine.value_load(t.near[0:1, 0:1], min_val=0, max_val=1)
            with engine.If(near):
                program(True)
            with engine.Else():
                program(False)

        with nc.Block() as block:
            @block.sync
            def _(sp):
                def load_window(i, u):
                    wait_used(sp, multiplied[u], i)
                    base = sp.value_load(t.window_base[0:1, ds(i * U + u, 1)], min_val=0,
                                         max_val=(NT - 1) * P)
                    sp.dma_start(window[:, u, :], t.bm[ds(base, P), :]).then_inc(window_loaded[u], 16)

                def program(near):
                    def body(i):
                        for u in range(U):
                            wait_used(sp, turned[u], i)
                            sp.dma_start(feat[:, u, :], feat_d[ds(i * U + u, 1), :, :].rearrange(
                                "a p f -> (a p) f")).then_inc(feat_loaded[u], 16)
                            if near:
                                load_window(i, u)
                    repeat(sp, N_IT - 1, body)
                    for u in range(U):
                        g = (N_IT - 1) * U + u
                        sp.wait_ge(turned[u], N_IT - 1)
                        if g < pl.WHOLE:
                            sp.dma_start(feat[:, u, :], feat_d[g, :, :]).then_inc(feat_loaded[u], 16)
                        else:
                            sp.dma_start(feat[0:rest_p, u, :], t.edge_attr[g * GROUP:pl.E, :].rearrange(
                                "(p j) f -> p (j f)", j=J)).then_inc(feat_loaded[u], 16)
                        if near:
                            load_window(N_IT - 1, u)

                by_kind(sp, program)

            @block.gpsimd
            def _(pool):
                last_node = pool.to_reg(NT * P - 1)
                last_row = pool.to_reg(pl.E - 1)
                regs = [pool.alloc_register(n) for n in ("after", "after2")]

                def gather(i, after, u):
                    pool.wait_ge(rows_cleared, 1)
                    pool.wait_ge(dst_ready[u], after)
                    wait_used(pool, rows_ready[u], i)
                    for j in range(J):
                        nc.gpsimd.indirect_dma_start(
                            out=got[:, u, j * 2 * D:(j + 1) * 2 * D], out_offset=None,
                            in_=t.bm[:, :],
                            in_offset=bass.IndirectOffsetOnAxis(ap=dst_now[:, u, j:j + 1], axis=0),
                            bounds_check=last_node, oob_is_err=False).then_inc(gathered[u], 16)

                def scatter(after, u):
                    pool.wait_ge(rows_cleared, 1)
                    pool.wait_ge(place_ready[u], after)
                    pool.wait_ge(ids_ready[u], after)
                    pool.wait_ge(rows_ready[u], after)
                    for j in range(J):
                        nc.gpsimd.indirect_dma_start(
                            out=t.rows[:, :],
                            out_offset=bass.IndirectOffsetOnAxis(ap=place[:, u, j:j + 1], axis=0),
                            in_=rows[:, u, j * pl.ROW:(j + 1) * pl.ROW], in_offset=None,
                            bounds_check=last_row, oob_is_err=False).then_inc(scattered[u], 16)

                nc.gpsimd.memset(rows[:, :, :], 0.0).then_inc(rows_cleared, 1)

                def program(near):
                    if near:
                        def body(i):
                            after = held(pool, regs[0], i, 1)
                            scatter(after, 0)
                            scatter(after, 1)
                        repeat(pool, N_IT, body)
                        return
                    gather(0, 1, 0)
                    def body(i):
                        after, after2 = held(pool, regs[0], i, 1), held(pool, regs[1], i, 2)
                        gather(i, after, 1)
                        scatter(after, 0)
                        gather(after, after2, 0)
                        scatter(after, 1)
                    repeat(pool, N_IT - 1, body)
                    gather(N_IT - 1, N_IT, 1)
                    scatter(N_IT, 0)
                    scatter(N_IT, 1)

                by_kind(pool, program)
                for u in range(U):
                    pool.wait_ge(scattered[u], 16 * J * N_IT)

            @block.scalar
            def _(act):
                def turned_feat(i, u):
                    act.wait_ge(turned[u], i + 1)
                    wait_used(act, multiplied[u], i)
                    nc.scalar.copy(feat_t[:, u, :], turn_ps[u]).then_inc(turned_copied[u], 1)

                def turned_hot(i, u):
                    act.wait_ge(dst_hot_turned[u], i + 1)
                    wait_used(act, multiplied[u], i)
                    nc.scalar.copy(dst_hot_t[:, u, :], hot_ps).then_inc(dst_hot_copied[u], 1)

                def to_rows(i, u):
                    act.wait_ge(multiplied[u], i + 1)
                    wait_used(act, scattered[u], i * (16 * J))
                    nc.scalar.copy(rows_view(u), prod_view(u)).then_inc(rows_ready[u], 1)

                def program(near):
                    if near:
                        staggered(act, N_IT, [(0, turned_feat), (0, turned_hot), (1, to_rows)], U)
                    else:
                        staggered(act, N_IT, [(0, turned_feat)], U)

                act.wait_ge(rows_cleared, 1)
                by_kind(act, program)

            @block.tensor
            def _(pe):
                def turn_feat(i, u):
                    pe.wait_ge(feat_loaded[u], i * 16 + 16)
                    wait_used(pe, turned_copied[u], i)
                    for j in range(J):
                        last = nc.tensor.transpose(turn_ps[u][:, j * P:(j + 1) * P],
                                                   feat[:, u, j * D:(j + 1) * D], t.ident[:, :])
                    last.then_inc(turned[u], 1)

                def turn_hot(i, u):
                    pe.wait_ge(dst_hot_ready[u], i + 1)
                    wait_last_group(pe, dst_hot_copied, i, u)
                    for j in range(J):
                        last = nc.tensor.transpose(hot_ps[:, j * P:(j + 1) * P],
                                                   dst_hot[:, u, j * P:(j + 1) * P], t.ident_bf[:, :])
                    last.then_inc(dst_hot_turned[u], 1)

                def rank_edges(i, u):
                    c0 = (i * U + u) * JN
                    pe.wait_ge(before_ready[u], i + 1)
                    wait_last_group(pe, picked, i, u)
                    nc.tensor.matmul(rank_ps, t.before_bf[:, :], hot[:, ds(c0, JN)],
                                     start=True, stop=False)
                    for j in range(J - 1):
                        for k in range(j + 1, J):
                            nc.tensor.matmul(rank_ps[:, k * NT:(k + 1) * NT], t.ones_bf[:, :],
                                             hot[:, ds(c0 + j * NT, NT)], start=False, stop=False)
                    nc.tensor.matmul(rank_ps.rearrange("p (j b) -> p j b", j=J), t.ones[:, :],
                                     under(before[:, u, :], J), start=False,
                                     stop=True).then_inc(ranked[u], 1)

                def product(i, u, near):
                    pe.wait_ge(turned_copied[u], i + 1)
                    if near:
                        pe.wait_ge(dst_hot_copied[u], i + 1)
                        pe.wait_ge(window_loaded[u], i * 16 + 16)
                    wait_used(pe, rows_ready[u], i)
                    for j in range(J):
                        to = prod_ps[u][:, j // 2, (j % 2) * 2 * D:(j % 2 + 1) * 2 * D]
                        last = nc.tensor.matmul(to, feat_t[:, u, j * P:(j + 1) * P],
                                                t.w_edge[:, :], start=True, stop=not near)
                        if near:
                            last = nc.tensor.matmul(to, dst_hot_t[:, u, j * P:(j + 1) * P],
                                                    window[:, u, :], start=False, stop=True)
                    last.then_inc(multiplied[u], 1)

                def program(near):
                    steps = [(0, turn_feat)] + [(0, turn_hot)] * near
                    steps += [(0, rank_edges), (1, lambda i, u: product(i, u, near))]
                    staggered(pe, N_IT, steps, U)

                by_kind(pe, program)

            @block.vector
            def _(dve):
                v = nc.vector
                v.tensor_scalar(before[:, 0, :], t.start[:, :], 1.0 / P, None,
                                ALU.mult).then_inc(before_ready[0], 1)
                for u in range(U):
                    v.tensor_copy(dst_now[:, u, :], t.dst_i[:, u * J:(u + 1) * J]).then_inc(dst_ready[u], 1)
                dve.wait_ge(rows_cleared, 1)

                def one_hot(i, u):
                    wait_used(dve, dst_hot_turned[u], i)
                    v.tensor_tensor(dst_hot[:, u, :].rearrange("p (j n) -> p j n", j=J),
                                    over(t.dst_rel[:, ds((i * U + u) * J, J)], P),
                                    under(t.lane_bf[:, :], J), ALU.is_equal).then_inc(dst_hot_ready[u], 1)

                def count_on(i, u):
                    nxt, more = (u + 1) % U, (u + 1) // U
                    col = (i * U + u) * J
                    wait_used(dve, ranked[nxt], i + more)
                    v.tensor_reduce(group_hot[:, u, :], hot[:, ds(col * NT, JN)].rearrange(
                        "p (j b) -> p b j", j=J), AX.X, ALU.add).then_inc(hot_summed[u], 1)
                    dve.wait_ge(hot_summed[u], i + 1)
                    dve.wait_ge(before_ready[u], i + 1)
                    v.tensor_tensor(before[:, nxt, :], before[:, u, :], group_hot[:, u, :],
                                    ALU.add).then_inc(before_ready[nxt], 1)

                def find_place(i, u):
                    col = (i * U + u) * J
                    dve.wait_ge(ranked[u], i + 1)
                    v.tensor_tensor(rank[:, u, :], rank_ps, hot[:, ds(col * NT, JN)],
                                    ALU.mult).then_inc(picked[u], 1)
                    dve.wait_ge(picked[u], i + 1)
                    v.tensor_reduce(place_f[:, u, :], rank[:, u, :].rearrange(
                        "p (j b) -> p j b", j=J), AX.X, ALU.add).then_inc(place_sum[u], 1)
                    dve.wait_ge(place_sum[u], i + 1)
                    wait_used(dve, scattered[u], i * (16 * J))
                    v.tensor_tensor(place[:, u, :], place_f[:, u, :], t.pad_off[:, ds(col, J)],
                                    ALU.add).then_inc(place_ready[u], 1)
                    v.tensor_copy(rows[:, u, D:J * pl.ROW:pl.ROW],
                                  t.id1[:, ds(col, J)]).then_inc(ids_ready[u], 1)

                def add_gathered(i, u):
                    dve.wait_ge(multiplied[u], i + 1)
                    dve.wait_ge(gathered[u], i * (16 * J) + 16 * J)
                    v.tensor_tensor(rows_view(u), prod_view(u),
                                    got[:, u, :].rearrange("p (k f) -> p k f", f=D),
                                    ALU.add).then_inc(rows_ready[u], 1)
                    v.tensor_copy(dst_now[:, u, :], t.dst_i[:, ds((i * U + u) * J + U * J, J)]
                                  ).then_inc(dst_ready[u], 1)

                def program(near):
                    if near:
                        staggered(dve, N_IT, [(0, one_hot), (0, count_on), (1, find_place)], U)
                    else:
                        staggered(dve, N_IT, [(0, count_on), (1, find_place), (1, add_gathered)], U)

                by_kind(dve, program)


def load_units(nc, pl, t, sp, i, u, to, first, width, loaded):
    for q in range(Q):
        row = sp.value_load(t.unit_row[0:1, ds((i * R + u) * Q + q, 1)], min_val=0, max_val=pl.E)
        sp.dma_start(to[:, u, q * K * width:(q + 1) * K * width].rearrange("p (k f) -> p k f", k=K),
                     t.rows[ds(row, K * P), first:first + width].rearrange("(p k) f -> p k f", k=K)
                     ).then_inc(loaded[u], 16)


def logits(nc, pl, t):
    D, H, HD, H2 = pl.D, pl.H, pl.HD, pl.HALF
    N_IT = pl.SG // R
    with ExitStack() as ctx:
        def sb(name, shape, dt=F32):
            return ctx.enter_context(nc.sbuf_tensor(name, shape, dt))

        def sems(name):
            return [t.semaphore(f"{name}{u}") for u in range(R)]

        half = sb("half", [P, R, J * H2])
        one = sb("one", [P, R, J * P])
        one_t = sb("one_t", [P, R, J * P])
        hid = sb("hid", [P, R, J * D])
        loaded, rel_ready, one_ready, one_turned, one_t_ready = map(
            sems, ("half_loaded", "rel_ready", "one_ready", "one_turned", "one_t_ready"))
        summed, copied, leaky, scaled, logit_ready = map(
            sems, ("hidden_summed", "hidden_copied", "leaky_ready", "hidden_scaled", "logit_ready"))
        turn_ps = [t.psum[:, u, :] for u in range(R)]
        hid_ps = [t.psum[:, R + u, :] for u in range(R)]

        with nc.Block() as block:
            @block.sync
            def _(sp):
                def load(i, u):
                    wait_used(sp, summed[u], i)
                    load_units(nc, pl, t, sp, i, u, half, 0, H2, loaded)

                staggered(sp, N_IT, [(0, load)])

            @block.tensor
            def _(pe):
                def turn(i, u):
                    pe.wait_ge(one_ready[u], i + 1)
                    wait_used(pe, one_t_ready[u], i)
                    for j in range(J):
                        last = nc.tensor.transpose(turn_ps[u][:, j * P:(j + 1) * P],
                                                   one[:, u, j * P:(j + 1) * P], t.ident[:, :])
                    last.then_inc(one_turned[u], 1)

                def hidden(i, u):
                    pe.wait_ge(one_t_ready[u], i + 1)
                    wait_used(pe, copied[u], i)
                    for j in range(J):
                        if j % K == 0:
                            b = pe.value_load(t.unit_bucket[0:1, ds((i * R + u) * Q + j // K, 1)],
                                              min_val=0, max_val=pl.NT - 1)
                        to = hid_ps[u][:, j * D:(j + 1) * D]
                        nc.tensor.matmul(to, one_t[:, u, j * P:(j + 1) * P],
                                         t.node_a[:, ds(b * D, D)], start=True, stop=False)
                        last = nc.tensor.matmul(to, t.ident[:, :], half[:, u, j * H2:j * H2 + D],
                                                start=False, stop=True)
                    last.then_inc(summed[u], 1)

                staggered(pe, N_IT, [(0, turn), (1, hidden)])

            @block.scalar
            def _(act):
                def copy_one(i, u):
                    act.wait_ge(one_turned[u], i + 1)
                    wait_used(act, summed[u], i)
                    nc.scalar.copy(one_t[:, u, :], turn_ps[u]).then_inc(one_t_ready[u], 1)

                def copy_hidden(i, u):
                    act.wait_ge(summed[u], i + 1)
                    wait_used(act, logit_ready[u], i)
                    nc.scalar.copy(hid[:, u, :], hid_ps[u]).then_inc(copied[u], 1)

                staggered(act, N_IT, [(0, copy_one), (1, copy_hidden)])

            @block.gpsimd
            def _(pool):
                def scale(i, u):
                    pool.wait_ge(leaky[u], i + 1)
                    for j in range(J):
                        h = hid[:, u, j * D:(j + 1) * D]
                        last = nc.gpsimd.tensor_tensor(h, h, t.attn[:, :], ALU.mult)
                    last.then_inc(scaled[u], 1)

                staggered(pool, N_IT, [(0, scale)])

            @block.vector
            def _(dve):
                v = nc.vector

                def one_hot(i, u):
                    col = (i * R + u) * J
                    dve.wait_ge(loaded[u], i * (16 * Q) + 16 * Q)
                    v.tensor_tensor(t.rel[:, ds(col, J)], half[:, u, D:J * H2:H2],
                                    t.tile_base[:, ds(col, J)], ALU.subtract).then_inc(rel_ready[u], 1)
                    dve.wait_ge(rel_ready[u], i + 1)
                    wait_used(dve, one_turned[u], i)
                    v.tensor_tensor(one[:, u, :].rearrange("p (j n) -> p j n", j=J),
                                    over(t.rel[:, ds(col, J)], P), under(t.lane[:, :], J),
                                    ALU.is_equal).then_inc(one_ready[u], 1)

                def leak(i, u):
                    dve.wait_ge(copied[u], i + 1)
                    v.scalar_tensor_tensor(hid[:, u, :], hid[:, u, :], SLOPE, hid[:, u, :],
                                           ALU.mult, ALU.max).then_inc(leaky[u], 1)

                def head_sums(i, u):
                    dve.wait_ge(scaled[u], i + 1)
                    v.tensor_reduce(t.logits[:, ds((i * R + u) * J * H, J * H)],
                                    hid[:, u, :].rearrange("p (k d) -> p k d", d=HD),
                                    AX.X, ALU.add).then_inc(logit_ready[u], 1)

                staggered(dve, N_IT, [(0, one_hot), (2, leak), (3, head_sums)])


def spread_of_logits(nc, pl, t):
    H, ST = pl.H, pl.ST
    with ExitStack() as ctx:
        def sb(name, shape, dt=F32):
            return ctx.enter_context(nc.sbuf_tensor(name, shape, dt))

        def sem(name):
            return t.semaphore(name)

        below0 = sb("below0", [P, ST])
        bar = sb("bar", [P, ST])
        ends = sb("extremes", [P, 2, H])
        tops = sb("tops", [H, 2])
        gap = sb("gap", [H, 1])
        diag = sb("diag", [H, H])
        wide_f = sb("wide_f", [1, 1])
        order = sem("spread_order")
        ends_ready, ends_turned, diag_ready, top_ready, wide_ready = map(
            sem, ("ends_ready", "ends_turned", "diag_ready", "top_ready", "wide_ready"))
        ends_ps = t.psum[0:H, 0, 0:2 * P].rearrange("h (k p) -> h k p", k=2)
        top_ps = t.psum[:, 1, 0:H]
        gap_ps = t.psum[0:1, 2, 0:H]
        masked = t.masked.rearrange("p (t h) -> p t h", h=H)
        all_logits = t.logits.rearrange("p (t h) -> p t h", h=H)

        with nc.Block() as block:
            @block.tensor
            def _(pe):
                pe.wait_ge(ends_ready, 1)
                for k in range(2):
                    last = nc.tensor.transpose(ends_ps[:, k, :], ends[:, k, :], t.ident[:, :])
                last.then_inc(ends_turned, 1)
                pe.wait_ge(diag_ready, 1)
                nc.tensor.matmul(top_ps, t.ones[0:H, :], diag[:, :], start=True, stop=True)
                nc.tensor.matmul(gap_ps, gap[:, :], t.ident[0:H, 0:H],
                                 start=True, stop=True).then_inc(top_ready, 1)

            @block.vector
            def _(dve):
                v = nc.vector
                chain = Chain(dve, order)
                v.tensor_scalar(below0[:, :], t.rel[:, :], 0.0, NEG, ALU.is_lt, ALU.mult)
                chain.then(v.tensor_scalar(bar[:, :], t.rel[:, :], float(P), NEG, ALU.is_ge, ALU.mult))
                chain.then(v.tensor_tensor(bar[:, :], bar[:, :], below0[:, :], ALU.add))
                for k, op in enumerate((ALU.add, ALU.subtract)):
                    a, b = (all_logits, over(bar[:, :], H)) if k == 0 else (over(bar[:, :], H), all_logits)
                    chain.then(v.tensor_tensor(masked, a, b, op))
                    chain.then(v.tensor_reduce(ends[:, k, :], masked.rearrange("p t h -> p h t"),
                                               AX.X, ALU.max))
                v.tensor_copy(below0[:, 0:1], bar[:, 0:1]).then_inc(ends_ready, 1)
                dve.wait_ge(ends_turned, 1)
                chain.then(v.tensor_reduce(tops[:, :], ends_ps, AX.X, ALU.max))
                chain.then(v.tensor_tensor(gap[:, :], tops[:, 0:1], tops[:, 1:2], ALU.add))
                v.tensor_scalar(diag[:, :], t.ident[0:H, 0:H], tops[:, 0:1], None,
                                ALU.mult).then_inc(diag_ready, 1)
                dve.wait_ge(top_ready, 1)
                chain.then(v.tensor_copy(t.top[:, :], top_ps))
                chain.then(v.tensor_reduce(wide_f[:, :], gap_ps, AX.X, ALU.max))
                chain.then(v.tensor_scalar(wide_f[:, :], wide_f[:, :], SPAN, None, ALU.is_le))
                chain.then(v.tensor_scalar(wide_f[:, :], wide_f[:, :], -1.0, 1.0, ALU.mult, ALU.add))
                chain.then(v.tensor_copy(t.wide[:, :], wide_f[:, :]))


def maxima(nc, pl, t):
    H, ST = pl.H, pl.ST
    with ExitStack() as ctx:
        def sb(name, shape, dt=F32):
            return ctx.enter_context(nc.sbuf_tensor(name, shape, dt))

        def sem(name):
            return t.semaphore(name)

        def sems(name):
            return [sem(f"{name}{u}") for u in range(U)]

        barred = sb("barred", [P, U, P])
        spread = sb("spread", [P, U, H * P])
        new_up = sb("new_up", [P, ST])
        new_down = sb("new_down", [P, ST])
        one = sb("one_m", [P, U, P])
        one_t = sb("one_tm", [P, U, P])
        barred_ready, spread_ready, spread_turned, tile_done = map(
            sems, ("barred_ready", "spread_ready", "spread_turned", "tile_max_ready"))
        one_ready, one_turned, one_t_ready, max_ready, below_ready, capped = map(
            sems, ("one_m_ready", "one_m_turned", "one_tm_ready", "edge_max_ready", "below_ready",
                   "capped"))
        order = sem("max_order")
        turn_ps = [t.psum[:, 2 * u:2 * u + 2, :] for u in range(U)]
        one_ps = [t.psum[:, 4 + u, 0:P] for u in range(U)]
        max_ps = [t.psum[:, 6 + u, 0:H] for u in range(U)]
        HB = 512 // P
        N_IT = ST // U

        with nc.Block() as block:
            @block.tensor
            def _(pe):
                wide = pe.value_load(t.wide[0:1, 0:1], min_val=0, max_val=1)
                with pe.If(wide):
                    def turn(i):
                        for u in range(U):
                            pe.wait_ge(spread_ready[u], i + 1)
                            wait_used(pe, tile_done[u], i)
                            for h in range(H):
                                last = nc.tensor.transpose(
                                    turn_ps[u][:, h // HB, (h % HB) * P:(h % HB + 1) * P],
                                    spread[:, u, h * P:(h + 1) * P], t.ident[:, :])
                            last.then_inc(spread_turned[u], 1)

                    repeat(pe, N_IT, turn)

                    def pick(i):
                        for u in range(U):
                            pe.wait_ge(one_ready[u], i + 1)
                            wait_used(pe, one_t_ready[u], i)
                            nc.tensor.transpose(one_ps[u], one[:, u, :],
                                                t.ident[:, :]).then_inc(one_turned[u], 1)
                        for u in range(U):
                            pe.wait_ge(one_t_ready[u], i + 1)
                            wait_used(pe, below_ready[u], i)
                            nc.tensor.matmul(max_ps[u], one_t[:, u, :],
                                             t.node_max[:, :, ds(i * U + u, 1)],
                                             start=True, stop=True).then_inc(max_ready[u], 1)

                    repeat(pe, N_IT, pick)

            @block.scalar
            def _(act):
                wide = act.value_load(t.wide[0:1, 0:1], min_val=0, max_val=1)
                with act.If(wide):
                    def copy(i):
                        for u in range(U):
                            act.wait_ge(one_turned[u], i + 1)
                            wait_used(act, max_ready[u], i)
                            nc.scalar.copy(one_t[:, u, :], one_ps[u]).then_inc(one_t_ready[u], 1)

                    repeat(act, N_IT, copy)

            @block.vector
            def _(dve):
                v = nc.vector
                wide = dve.value_load(t.wide[0:1, 0:1], min_val=0, max_val=1)
                with dve.If(wide):
                    def tile_maxima(i):
                        for u in range(U):
                            tile = i * U + u
                            wait_used(dve, spread_ready[u], i)
                            v.tensor_scalar(barred[:, u, :], t.lane[:, :], t.rel[:, ds(tile, 1)], NEG,
                                            ALU.not_equal, ALU.mult).then_inc(barred_ready[u], 1)
                            dve.wait_ge(barred_ready[u], i + 1)
                            wait_used(dve, spread_turned[u], i)
                            v.tensor_tensor(spread[:, u, :].rearrange("p (h n) -> p h n", h=H),
                                            over(t.logits[:, ds(tile * H, H)], P),
                                            under(barred[:, u, :], H), ALU.add).then_inc(spread_ready[u], 1)
                        for u in range(U):
                            tile = i * U + u
                            dve.wait_ge(spread_turned[u], i + 1)
                            v.tensor_reduce(t.tile_max[:, :, ds(tile, 1)],
                                            turn_ps[u].rearrange("p b (k e) -> p (b k) e", e=P),
                                            AX.X, ALU.max).then_inc(tile_done[u], 1)

                    repeat(dve, N_IT, tile_maxima)
                    for u in range(U):
                        dve.wait_ge(tile_done[u], N_IT)
                    chain = Chain(dve, order)
                    v.memset(new_up[:, 0:1], 0.0)
                    v.memset(new_down[:, ST - 1:ST], 0.0)
                    v.tensor_tensor(new_up[:, 1:ST], t.tile_base[:, 1:ST], t.tile_base[:, 0:ST - 1],
                                    ALU.not_equal)
                    chain.then(v.tensor_tensor(new_down[:, 0:ST - 1], t.tile_base[:, 1:ST],
                                               t.tile_base[:, 0:ST - 1], ALU.not_equal))
                    v.tensor_scalar(new_up[:, :], new_up[:, :], NEG, None, ALU.mult)
                    chain.then(v.tensor_scalar(new_down[:, :], new_down[:, :], NEG, None, ALU.mult))
                    for h in range(H):
                        last = v.tensor_tensor_scan(t.node_max[:, h, :], new_up[:, :],
                                                    t.tile_max[:, h, :], NEG, ALU.add, ALU.max)
                    chain.then(last)
                    for h in range(H):
                        last = v.tensor_tensor_scan(t.tile_max[:, h, ::-1], new_down[:, ::-1],
                                                    t.tile_max[:, h, ::-1], NEG, ALU.add, ALU.max)
                    chain.then(last)
                    chain.then(v.tensor_tensor(t.node_max[:, :, :], t.node_max[:, :, :],
                                               t.tile_max[:, :, :], ALU.max))

                    def take_off(i):
                        for u in range(U):
                            wait_used(dve, one_turned[u], i)
                            v.tensor_scalar(one[:, u, :], t.lane[:, :], t.rel[:, ds(i * U + u, 1)],
                                            None, ALU.is_equal).then_inc(one_ready[u], 1)
                        for u in range(U):
                            at = ds((i * U + u) * H, H)
                            dve.wait_ge(max_ready[u], i + 1)
                            v.tensor_tensor(t.below[:, at], t.logits[:, at], max_ps[u],
                                            ALU.subtract).then_inc(below_ready[u], 1)
                            dve.wait_ge(below_ready[u], i + 1)
                            v.tensor_scalar(t.below[:, at], t.below[:, at], 0.0, None,
                                            ALU.min).then_inc(capped[u], 1)

                    repeat(dve, N_IT, take_off)
                    for u in range(U):
                        dve.wait_ge(capped[u], N_IT)
                with dve.Else():
                    v.tensor_tensor(t.below.rearrange("p (t h) -> p t h", h=H),
                                    t.logits.rearrange("p (t h) -> p t h", h=H),
                                    under(t.top[:, :], ST), ALU.subtract).then_inc(order, 1)
                    dve.wait_ge(order, 1)
                    v.tensor_scalar(t.below, t.below, 0.0, None, ALU.min)


def sums(nc, pl, t):
    D, H, HD, H2, WM = pl.D, pl.H, pl.HD, pl.HALF, pl.WM
    N_IT = pl.SG // R
    with ExitStack() as ctx:
        def sb(name, shape, dt=F32):
            return ctx.enter_context(nc.sbuf_tensor(name, shape, dt))

        def sem(name):
            return t.semaphore(name)

        def sems(name):
            return [sem(f"{name}{u}") for u in range(R)]

        msg = sb("msg", [P, R, J * D])
        one = sb("one_s", [P, R, J * P])
        wm = sb("wm", [P, R, J * WM])
        loaded, one_ready, exp_ready, wm_ready, tile_summed = map(
            sems, ("msg_loaded", "one_s_ready", "exp_ready", "wm_ready", "tile_summed"))
        added = sem("added")
        sum_ps = [t.psum[:, u, 0:Q * WM] for u in range(R)]

        with nc.Block() as block:
            @block.sync
            def _(sp):
                def load(i, u):
                    wait_used(sp, wm_ready[u], i)
                    load_units(nc, pl, t, sp, i, u, msg, H2, D, loaded)

                staggered(sp, N_IT, [(0, load)])

            @block.scalar
            def _(act):
                def exp(i, u):
                    wait_used(act, tile_summed[u], i)
                    nc.scalar.activation(
                        wm[:, u, :].rearrange("p (j f) -> p j f", j=J)[:, :, D:WM],
                        t.below[:, ds((i * R + u) * J * H, J * H)].rearrange("p (j h) -> p j h", j=J),
                        ACT.Exp).then_inc(exp_ready[u], 1)

                staggered(act, N_IT, [(0, exp)])

            @block.gpsimd
            def _(pool):
                def weigh(i, u):
                    pool.wait_ge(loaded[u], i * (16 * Q) + 16 * Q)
                    pool.wait_ge(exp_ready[u], i + 1)
                    for j in range(J):
                        last = nc.gpsimd.tensor_tensor(
                            wm[:, u, j * WM:j * WM + D].rearrange("p (h d) -> p h d", d=HD),
                            msg[:, u, j * D:(j + 1) * D].rearrange("p (h d) -> p h d", d=HD),
                            over(wm[:, u, j * WM + D:(j + 1) * WM], HD), ALU.mult)
                    last.then_inc(wm_ready[u], 1)

                staggered(pool, N_IT, [(0, weigh)])

            @block.tensor
            def _(pe):
                def per_node(i, u):
                    pe.wait_ge(one_ready[u], i + 1)
                    pe.wait_ge(wm_ready[u], i + 1)
                    wait_used(pe, added, (i * R + u) * Q)
                    for j in range(J):
                        last = nc.tensor.matmul(
                            sum_ps[u][:, (j // K) * WM:(j // K + 1) * WM],
                            one[:, u, j * P:(j + 1) * P], wm[:, u, j * WM:(j + 1) * WM],
                            start=j % K == 0, stop=j % K == K - 1)
                    last.then_inc(tile_summed[u], 1)

                staggered(pe, N_IT, [(0, per_node)])

            @block.vector
            def _(dve):
                v = nc.vector
                v.memset(t.nodes_flat[:, :], 0.0).then_inc(added, Q * (R - 1))

                def one_hot(i, u):
                    wait_used(dve, tile_summed[u], i)
                    v.tensor_tensor(one[:, u, :].rearrange("p (j n) -> p j n", j=J),
                                    over(t.rel[:, ds((i * R + u) * J, J)], P),
                                    under(t.lane[:, :], J), ALU.is_equal).then_inc(one_ready[u], 1)

                def add(i, u):
                    dve.wait_ge(tile_summed[u], i + 1)
                    for q in range(Q):
                        unit = (i * R + u) * Q + q
                        b = dve.value_load(t.unit_bucket[0:1, ds(unit, 1)], min_val=0,
                                           max_val=pl.NT - 1)
                        acc = t.nodes_flat[:, ds(b * WM, WM)]
                        dve.wait_ge(added, unit + Q * (R - 1))
                        v.tensor_tensor(acc, acc, sum_ps[u][:, q * WM:(q + 1) * WM],
                                        ALU.add).then_inc(added, 1)

                staggered(dve, N_IT, [(0, one_hot), (2, add)])


def output(nc, pl, t):
    D, H, HD, WM, NT = pl.D, pl.H, pl.HD, pl.WM, pl.NT
    N_IT = NT // U
    with ExitStack() as ctx:
        def sb(name, shape, dt=F32):
            return ctx.enter_context(nc.sbuf_tensor(name, shape, dt))

        def sem(name):
            return t.semaphore(name)

        def sems(name):
            return [sem(f"{name}{u}") for u in range(U)]

        inv = sb("inv", [P, NT, H])
        xs = sb("xs", [P, NT * D])
        mean = sb("mean", [P, U, D])
        mean_t = sb("mean_t", [P, U, D])
        x_loaded = sem("x_again")
        x_biased = sem("x_biased")
        order = sem("out_order")
        mean_ready, mean_turned, mean_t_ready, projected, out_ready = map(
            sems, ("mean_ready", "mean_turned", "mean_t_ready", "out_projected", "out_ready"))
        stored = sem("out_stored")
        turn_ps = [t.psum[:, u, 0:D] for u in range(U)]
        proj_ps = [t.psum[:, 2 + u, 0:D] for u in range(U)]
        xv = xs[:, :].rearrange("p (t f) -> p t f", f=D)

        with nc.Block() as block:
            @block.sync
            def _(sp):
                sp.dma_start(xv[:, 0:pl.WHOLE_N, :], t.x[0:pl.WHOLE_N * P, :].rearrange(
                    "(t p) f -> p t f", p=P)).then_inc(x_loaded, 16)
                sp.wait_ge(x_biased, 1)
                sp.dma_start(xv[0:pl.REST_N, pl.WHOLE_N, :],
                             t.x[pl.WHOLE_N * P:pl.N, :]).then_inc(x_loaded, 16)
                for u in range(U):
                    sp.wait_ge(out_ready[u], N_IT)
                sp.dma_start(t.out[0:pl.WHOLE_N * P, :].rearrange("(t p) f -> p t f", p=P),
                             xv[:, 0:pl.WHOLE_N, :]).then_inc(stored, 16)
                sp.dma_start(t.out[pl.WHOLE_N * P:pl.N, :],
                             xv[0:pl.REST_N, pl.WHOLE_N, :]).then_inc(stored, 16)
                sp.wait_ge(stored, 32)

            @block.tensor
            def _(pe):
                def body(i):
                    for u in range(U):
                        pe.wait_ge(mean_ready[u], i + 1)
                        wait_used(pe, mean_t_ready[u], i)
                        nc.tensor.transpose(turn_ps[u], mean[:, u, :], t.ident[:, :]).then_inc(mean_turned[u], 1)
                    for u in range(U):
                        pe.wait_ge(mean_t_ready[u], i + 1)
                        wait_used(pe, out_ready[u], i)
                        nc.tensor.matmul(proj_ps[u], mean_t[:, u, :], t.w_out[:, :],
                                         start=True, stop=True).then_inc(projected[u], 1)
                repeat(pe, N_IT, body)

            @block.scalar
            def _(act):
                def body(i):
                    for u in range(U):
                        act.wait_ge(mean_turned[u], i + 1)
                        wait_used(act, projected[u], i)
                        nc.scalar.copy(mean_t[:, u, :], turn_ps[u]).then_inc(mean_t_ready[u], 1)
                repeat(act, N_IT, body)

            @block.vector
            def _(dve):
                v = nc.vector
                chain = Chain(dve, order)
                v.memset(xv[:, pl.WHOLE_N:NT, :], 0.0).then_inc(x_biased, 1)
                chain.then(v.tensor_scalar(inv[:, :, :], t.nodes[:, :, D:WM], 1e-37, None, ALU.max))
                chain.then(v.reciprocal(inv[:, :, :], inv[:, :, :]))
                dve.wait_ge(x_loaded, 32)
                chain.then(v.tensor_tensor(xv[:, :, :], xv[:, :, :], under(t.out_bias[:, :], NT), ALU.add))
                inv_flat = inv[:, :, :].rearrange("p t h -> p (t h)")
                def body(i):
                    for u in range(U):
                        b = i * U + u
                        wait_used(dve, mean_turned[u], i)
                        v.tensor_tensor(mean[:, u, :].rearrange("p (h d) -> p h d", d=HD),
                                        t.nodes_flat[:, ds(b * WM, D)].rearrange("p (h d) -> p h d", d=HD),
                                        over(inv_flat[:, ds(b * H, H)], HD),
                                        ALU.mult).then_inc(mean_ready[u], 1)
                    for u in range(U):
                        b = i * U + u
                        dve.wait_ge(projected[u], i + 1)
                        v.tensor_tensor(xs[:, ds(b * D, D)], xs[:, ds(b * D, D)], proj_ps[u],
                                        ALU.add).then_inc(out_ready[u], 1)
                repeat(dve, N_IT, body)


def kernel(**inputs):
    import numpy as np
    from concourse import bacc
    from concourse.bass_utils import run_bass_kernel_spmd

    def arr(name):
        return np.asarray(inputs[name])

    D = arr("x").shape[1]
    msg_w = arr("L0_gnn_msg_w")
    arrays = {
        "x": arr("x"), "src": arr("src"), "dst": arr("dst"), "edge_attr": arr("edge_attr_128"),
        "w_node": np.concatenate([arr("L0_gnn_ni_w").T, arr("L0_gnn_nj_w").T, msg_w[:, :D].T], 1),
        "w_edge": np.concatenate([arr("L0_gnn_e_w").T, msg_w[:, D:].T], 1),
        "w_out": arr("L0_gnn_out_w").T,
        "ni_b": arr("L0_gnn_ni_b"), "nj_b": arr("L0_gnn_nj_b"), "e_b": arr("L0_gnn_e_b"),
        "msg_b": arr("L0_gnn_msg_b"), "out_b": arr("L0_gnn_out_b"),
        "attn": arr("L0_gnn_attn_proj").reshape(-1),
    }
    arrays = {k: np.ascontiguousarray(a) for k, a in arrays.items()}
    nc = bacc.Bacc("TRN2", target_bir_lowering=False, num_devices=1)
    aps = [nc.dram_tensor("in_" + k, a.shape, mybir.dt.from_np(a.dtype), kind="ExternalInput").ap()
           for k, a in arrays.items()]
    out = nc.dram_tensor("out", arrays["x"].shape, F32, kind="ExternalOutput").ap()
    gnn_kernel(nc, *aps, out)
    r = run_bass_kernel_spmd(nc, [{"in_" + k: a for k, a in arrays.items()}], core_ids=[0])
    return r.results[0]["out"]
```
